# Optimizing a Trainium2 kernel written in Bass

```python
import numpy as np
import jax
import jax.numpy as jnp

def _softmax(x, axis=-1):
    return jax.nn.softmax(x, axis=axis)

def _gelu(x):
    return jax.nn.gelu(x, approximate=True)

def _silu(x):
    return jax.nn.silu(x)

def _sigmoid(x):
    return jax.nn.sigmoid(x)

def _layernorm(x, axis=-1, eps=1e-05):
    m = jnp.mean(x, axis=axis, keepdims=True)
    v = jnp.var(x, axis=axis, keepdims=True)
    return (x - m) / jnp.sqrt(v + eps)

def _scatter_add(tgt, idx, src, axis=0):
    return tgt.at[idx].add(src)

def _segment_sum(src, seg, n):
    return jax.ops.segment_sum(src, seg, n)
kernel_name = 'mk_xattn_seq_d1_seqx_r8_7872b5'

def setup_inputs(seed: int=0):
    np.random.seed(seed)
    _w = jnp.asarray

    def _rec_inputs():
        import jax
        import jax.numpy as jnp
        _rk = jax.random.key(seed)
        x = -0.0002928 + 1 * jax.random.normal(jax.random.fold_in(_rk, 1), (64, 64, 128), jnp.float32)
        _lenS = 64 - jax.random.randint(jax.random.fold_in(_rk, 7), (64,), 0, max(1, 64 // 4) + 1, jnp.int32)
        _lenS2 = 64 - jax.random.randint(jax.random.fold_in(_rk, 8), (64,), 0, max(1, 64 // 4) + 1, jnp.int32)
        _ctx_1024P = jax.random.normal(jax.random.fold_in(_rk, 11), (64, 16, 128), jnp.float32)
        _ctx_1024c = jax.random.dirichlet(jax.random.fold_in(_rk, 511), 0.3 * jnp.ones((16,), jnp.float32), (64, 64))
        _ctx_1024t = jnp.einsum('bsk,bkd->bsd', _ctx_1024c, _ctx_1024P)
        _ctx_1024t = _ctx_1024t * jax.lax.rsqrt(jnp.mean(jnp.square(_ctx_1024t)) + 1e-12) * 0.953939
        ctx_1024 = -1.39393e-06 + 0.999914 * (_ctx_1024t + 0.3 * jax.random.normal(jax.random.fold_in(_rk, 611), (64, 64, 128), jnp.float32))
        return (x, ctx_1024)
    x, ctx_1024 = _rec_inputs()

    def _L0_xattn_setup():
        import jax, jax.numpy as jnp
        import numpy as np
        B, S, SE, D, H, FF, E, K = (2, 256, 256, 128, 16, 512, 8, 2)
        HD = D // H

        def _layernorm(x, g, b):
            m = x.mean(-1, keepdims=True)
            v = ((x - m) ** 2).mean(-1, keepdims=True)
            return (x - m) / jnp.sqrt(v + 1e-05) * g + b

        def _attn(q_in, k_in, v_in, wq, bq, wk, bk, wv, bv, wo, bo, causal):
            Bq, Sq, Dm = q_in.shape
            Sk = k_in.shape[1]
            Q = (q_in @ wq + bq).reshape(Bq, Sq, H, HD)
            Kp = (k_in @ wk + bk).reshape(Bq, Sk, H, HD)
            V = (v_in @ wv + bv).reshape(Bq, Sk, H, HD)
            scores = jnp.einsum('bqhd,bkhd->bhqk', Q, Kp) / jnp.sqrt(jnp.float32(HD))
            if causal:
                mask = jnp.tril(jnp.ones((Sq, Sk), bool))
                scores = jnp.where(mask, scores, -jnp.inf)
            a = jax.nn.softmax(scores, axis=-1)
            o = jnp.einsum('bhqk,bkhd->bqhd', a, V).reshape(Bq, Sq, Dm)
            return o @ wo + bo

        def _moe(x, rw, rb, w1, b1, w2, b2):
            T = x.shape[0] * x.shape[1]
            xf = x.reshape(T, D)
            router_weights = jax.nn.softmax(xf @ rw + rb, axis=-1)
            topw, topi = jax.lax.top_k(router_weights, K)
            topw = jax.nn.softmax(topw, axis=-1)
            combine = jnp.zeros((T, E), xf.dtype).at[jnp.arange(T)[:, None], topi].add(topw)
            h = jax.nn.gelu(jnp.einsum('td,edf->etf', xf, w1) + b1[:, None, :], approximate=False)
            eo = jnp.einsum('etf,efd->etd', h, w2) + b2[:, None, :]
            out = jnp.einsum('etd,te->td', eo, combine)
            return out.reshape(x.shape)
        key = jax.random.key(seed)
        ks = jax.random.split(key, 32)
        w = lambda k, shape: jax.random.normal(k, shape, jnp.float32) * 0.02
        inp = {'x': jax.random.normal(ks[0], (B, S, D), jnp.float32), 'encoder_output': jax.random.normal(ks[1], (B, SE, D), jnp.float32), 'sa_wq': w(ks[2], (D, D)), 'sa_bq': jnp.zeros((D,), jnp.float32), 'sa_wk': w(ks[3], (D, D)), 'sa_bk': jnp.zeros((D,), jnp.float32), 'sa_wv': w(ks[4], (D, D)), 'sa_bv': jnp.zeros((D,), jnp.float32), 'sa_wo': w(ks[5], (D, D)), 'sa_bo': jnp.zeros((D,), jnp.float32), 'ca_wq': w(ks[6], (D, D)), 'ca_bq': jnp.zeros((D,), jnp.float32), 'ca_wk': w(ks[7], (D, D)), 'ca_bk': jnp.zeros((D,), jnp.float32), 'ca_wv': w(ks[8], (D, D)), 'ca_bv': jnp.zeros((D,), jnp.float32), 'ca_wo': w(ks[9], (D, D)), 'ca_bo': jnp.zeros((D,), jnp.float32), 'ln1_g': jnp.ones((D,), jnp.float32), 'ln1_b': jnp.zeros((D,), jnp.float32), 'ln2_g': jnp.ones((D,), jnp.float32), 'ln2_b': jnp.zeros((D,), jnp.float32), 'ln3_g': jnp.ones((D,), jnp.float32), 'ln3_b': jnp.zeros((D,), jnp.float32), 'router_w': w(ks[10], (D, E)), 'router_b': jnp.zeros((E,), jnp.float32), 'e_w1': w(ks[11], (E, D, FF)), 'e_b1': jnp.zeros((E, FF), jnp.float32), 'e_w2': w(ks[12], (E, FF, D)), 'e_b2': jnp.zeros((E, D), jnp.float32)}
        return inp
    _L0_xattn_all = _L0_xattn_setup()
    _L0_xattn_in = {k: v for k, v in _L0_xattn_all.items() if k in ('sa_wq', 'sa_bq', 'sa_wk', 'sa_bk', 'sa_wv', 'sa_bv', 'sa_wo', 'sa_bo', 'ca_wq', 'ca_bq', 'ca_wk', 'ca_bk', 'ca_wv', 'ca_bv', 'ca_wo', 'ca_bo', 'ln1_g', 'ln1_b', 'ln2_g', 'ln2_b', 'ln3_g', 'ln3_b', 'router_w', 'router_b', 'e_w1', 'e_b1', 'e_w2', 'e_b2')}
    del _L0_xattn_all
    return {'x': x, 'ctx_1024': ctx_1024, 'L0_xattn_sa_wq': _L0_xattn_in['sa_wq'], 'L0_xattn_sa_bq': _L0_xattn_in['sa_bq'], 'L0_xattn_sa_wk': _L0_xattn_in['sa_wk'], 'L0_xattn_sa_bk': _L0_xattn_in['sa_bk'], 'L0_xattn_sa_wv': _L0_xattn_in['sa_wv'], 'L0_xattn_sa_bv': _L0_xattn_in['sa_bv'], 'L0_xattn_sa_wo': _L0_xattn_in['sa_wo'], 'L0_xattn_sa_bo': _L0_xattn_in['sa_bo'], 'L0_xattn_ca_wq': _L0_xattn_in['ca_wq'], 'L0_xattn_ca_bq': _L0_xattn_in['ca_bq'], 'L0_xattn_ca_wk': _L0_xattn_in['ca_wk'], 'L0_xattn_ca_bk': _L0_xattn_in['ca_bk'], 'L0_xattn_ca_wv': _L0_xattn_in['ca_wv'], 'L0_xattn_ca_bv': _L0_xattn_in['ca_bv'], 'L0_xattn_ca_wo': _L0_xattn_in['ca_wo'], 'L0_xattn_ca_bo': _L0_xattn_in['ca_bo'], 'L0_xattn_ln1_g': _L0_xattn_in['ln1_g'], 'L0_xattn_ln1_b': _L0_xattn_in['ln1_b'], 'L0_xattn_ln2_g': _L0_xattn_in['ln2_g'], 'L0_xattn_ln2_b': _L0_xattn_in['ln2_b'], 'L0_xattn_ln3_g': _L0_xattn_in['ln3_g'], 'L0_xattn_ln3_b': _L0_xattn_in['ln3_b'], 'L0_xattn_router_w': _L0_xattn_in['router_w'], 'L0_xattn_router_b': _L0_xattn_in['router_b'], 'L0_xattn_e_w1': _L0_xattn_in['e_w1'], 'L0_xattn_e_b1': _L0_xattn_in['e_b1'], 'L0_xattn_e_w2': _L0_xattn_in['e_w2'], 'L0_xattn_e_b2': _L0_xattn_in['e_b2']}

def reference(x, ctx_1024, L0_xattn_sa_wq, L0_xattn_sa_bq, L0_xattn_sa_wk, L0_xattn_sa_bk, L0_xattn_sa_wv, L0_xattn_sa_bv, L0_xattn_sa_wo, L0_xattn_sa_bo, L0_xattn_ca_wq, L0_xattn_ca_bq, L0_xattn_ca_wk, L0_xattn_ca_bk, L0_xattn_ca_wv, L0_xattn_ca_bv, L0_xattn_ca_wo, L0_xattn_ca_bo, L0_xattn_ln1_g, L0_xattn_ln1_b, L0_xattn_ln2_g, L0_xattn_ln2_b, L0_xattn_ln3_g, L0_xattn_ln3_b, L0_xattn_router_w, L0_xattn_router_b, L0_xattn_e_w1, L0_xattn_e_b1, L0_xattn_e_w2, L0_xattn_e_b2):
    import jax
    import jax.numpy as jnp

    def _L0_xattn_ref(x, encoder_output, sa_wq, sa_bq, sa_wk, sa_bk, sa_wv, sa_bv, sa_wo, sa_bo, ca_wq, ca_bq, ca_wk, ca_bk, ca_wv, ca_bv, ca_wo, ca_bo, ln1_g, ln1_b, ln2_g, ln2_b, ln3_g, ln3_b, router_w, router_b, e_w1, e_b1, e_w2, e_b2):
        import jax, jax.numpy as jnp
        import numpy as np
        B, S, SE, D, H, FF, E, K = (2, 256, 256, 128, 16, 512, 8, 2)
        HD = D // H

        def _layernorm(x, g, b):
            m = x.mean(-1, keepdims=True)
            v = ((x - m) ** 2).mean(-1, keepdims=True)
            return (x - m) / jnp.sqrt(v + 1e-05) * g + b

        def _attn(q_in, k_in, v_in, wq, bq, wk, bk, wv, bv, wo, bo, causal):
            Bq, Sq, Dm = q_in.shape
            Sk = k_in.shape[1]
            Q = (q_in @ wq + bq).reshape(Bq, Sq, H, HD)
            Kp = (k_in @ wk + bk).reshape(Bq, Sk, H, HD)
            V = (v_in @ wv + bv).reshape(Bq, Sk, H, HD)
            scores = jnp.einsum('bqhd,bkhd->bhqk', Q, Kp) / jnp.sqrt(jnp.float32(HD))
            if causal:
                mask = jnp.tril(jnp.ones((Sq, Sk), bool))
                scores = jnp.where(mask, scores, -jnp.inf)
            a = jax.nn.softmax(scores, axis=-1)
            o = jnp.einsum('bhqk,bkhd->bqhd', a, V).reshape(Bq, Sq, Dm)
            return o @ wo + bo

        def _moe(x, rw, rb, w1, b1, w2, b2):
            T = x.shape[0] * x.shape[1]
            xf = x.reshape(T, D)
            router_weights = jax.nn.softmax(xf @ rw + rb, axis=-1)
            topw, topi = jax.lax.top_k(router_weights, K)
            topw = jax.nn.softmax(topw, axis=-1)
            combine = jnp.zeros((T, E), xf.dtype).at[jnp.arange(T)[:, None], topi].add(topw)
            h = jax.nn.gelu(jnp.einsum('td,edf->etf', xf, w1) + b1[:, None, :], approximate=False)
            eo = jnp.einsum('etf,efd->etd', h, w2) + b2[:, None, :]
            out = jnp.einsum('etd,te->td', eo, combine)
            return out.reshape(x.shape)
        x = _layernorm(x + _attn(x, x, x, sa_wq, sa_bq, sa_wk, sa_bk, sa_wv, sa_bv, sa_wo, sa_bo, True), ln1_g, ln1_b)
        x = _layernorm(x + _attn(x, encoder_output, encoder_output, ca_wq, ca_bq, ca_wk, ca_bk, ca_wv, ca_bv, ca_wo, ca_bo, False), ln2_g, ln2_b)
        x = _layernorm(x + _moe(x, router_w, router_b, e_w1, e_b1, e_w2, e_b2), ln3_g, ln3_b)
        return x
    x = _L0_xattn_ref(x, ctx_1024, L0_xattn_sa_wq, L0_xattn_sa_bq, L0_xattn_sa_wk, L0_xattn_sa_bk, L0_xattn_sa_wv, L0_xattn_sa_bv, L0_xattn_sa_wo, L0_xattn_sa_bo, L0_xattn_ca_wq, L0_xattn_ca_bq, L0_xattn_ca_wk, L0_xattn_ca_bk, L0_xattn_ca_wv, L0_xattn_ca_bv, L0_xattn_ca_wo, L0_xattn_ca_bo, L0_xattn_ln1_g, L0_xattn_ln1_b, L0_xattn_ln2_g, L0_xattn_ln2_b, L0_xattn_ln3_g, L0_xattn_ln3_b, L0_xattn_router_w, L0_xattn_router_b, L0_xattn_e_w1, L0_xattn_e_b1, L0_xattn_e_w2, L0_xattn_e_b2)
    return x

_drawn_inputs = setup_inputs


def setup_inputs(seed=0):
    import zlib

    import numpy as np

    out = dict(_drawn_inputs(seed))
    spreads = {'L0_xattn_sa_bq': (0.0, 0.8),
     'L0_xattn_sa_bk': (0.0, 2.0),
     'L0_xattn_sa_bv': (0.0, 0.268),
     'L0_xattn_sa_bo': (0.0, 0.1),
     'L0_xattn_ca_bq': (0.0, 2.0),
     'L0_xattn_ca_bk': (0.0, 2.0),
     'L0_xattn_ca_bv': (0.0, 0.315),
     'L0_xattn_ca_bo': (0.0, 0.1),
     'L0_xattn_ln1_g': (1.0, 0.2),
     'L0_xattn_ln1_b': (0.0, 0.1),
     'L0_xattn_ln2_g': (1.0, 0.2),
     'L0_xattn_ln2_b': (0.0, 0.1),
     'L0_xattn_ln3_g': (1.0, 0.2),
     'L0_xattn_ln3_b': (0.0, 0.1),
     'L0_xattn_router_b': (0.0, 0.1),
     'L0_xattn_e_b1': (0.0, 0.516),
     'L0_xattn_e_b2': (0.0, 0.1)}
    factors = {'L0_xattn_sa_wq': 8.0,
     'L0_xattn_sa_wk': 8.0,
     'L0_xattn_sa_wv': 3.42,
     'L0_xattn_ca_wq': 8.0,
     'L0_xattn_ca_wk': 8.0}
    for name, (base, spread) in spreads.items():
        noise = np.random.default_rng([zlib.crc32(name.encode()), seed]).standard_normal(out[name].shape)
        drawn = base * np.exp(spread * noise) if base else spread * noise
        out[name] = jnp.asarray(drawn.astype(out[name].dtype))
    for name, factor in factors.items():
        out[name] = (out[name] * factor).astype(out[name].dtype)
    return out
```

```python
import numpy as np
import concourse.bass as bass
from concourse import mybir
from contextlib import ExitStack

B, S, D, H, FF, E = 64, 64, 128, 16, 512, 8
HD = D // H
P = 128
TOK = B * S
TILES = TOK // P
PAIRS = 2
BT = PAIRS * P
NBLK = TOK // BT
G = 4
J = H // G
HP = H // 2
SELF, CROSS = 0, 1
LAG = 2
EPS = 1e-5
MASKED = -1e30
FC = FF // P
MB = 512
MT = MB // P
ROUNDS = TOK // MB

C_ID, C_ONES, C_MKEY, C_MQRY, C_NEG, C_DELTA, C_HEAD, C_REV, C_END = np.cumsum(
    [0, P, P, S, P, 2 * S, S, J, E]).tolist()


def shape_constants():
    c = np.zeros((P, C_END), np.float32)
    p = np.arange(P)
    batch, tok = p // S, p % S
    same = batch[:, None] == batch[None, :]
    c[:, C_ID:C_ONES] = np.eye(P)
    c[:, C_ONES:C_MKEY] = same
    c[:, C_MKEY:C_MQRY] = np.where(np.arange(S)[None, :] > tok[:, None], MASKED, 0)
    c[:, C_MQRY:C_NEG] = np.where(same & (tok[None, :] > tok[:, None]), MASKED, 0)
    c[:, C_NEG:C_DELTA] = -np.repeat(tok[:, None] == np.arange(S)[None, :], 2, axis=1).astype(np.float32)
    c[:, C_DELTA:C_HEAD] = tok[:, None] == np.arange(S)[None, :]
    c[:, C_HEAD:C_REV] = (p[:, None] % 32) // HD == np.arange(J)[None, :]
    c[:, C_REV:C_END] = E - np.arange(E)[None, :]
    return c


class Block:

    def __init__(self, i, off):
        self.i, self.off, self.par = i, off, off % 2

    def back(self, d):
        return Block(self.i, self.off - d)

    def exists(self):
        return self.i is not None or 0 <= self.off < NBLK

    def times(self, m, add=0):
        return m * self.off + add if self.i is None else self.i * (2 * m) + (m * self.off + add)

    def landed(self, per=16):
        h = self.off // 2
        return (h + 1) * per if self.i is None else self.i * per + (h + 1) * per


class Unit:

    def __init__(self, kind, blk, pair):
        self.kind, self.blk, self.pair = kind, blk, pair
        self.buf = pair
        self.col = pair * P

    def count(self):
        return self.blk.times(2, self.pair + 1)

    def tile(self):
        return self.blk.times(2, self.pair)


def settle(eng, done, n, sem, value):
    value = value if isinstance(value, int) else eng.snap(value)
    eng.wait_ge(done, n)
    eng.wait_ge(sem, value)


def unit_at(now, slot):
    now = now.back(-(slot // 4))
    slot %= 4
    blk = now if slot < 2 else now.back(LAG)
    return Unit(SELF if slot < 2 else CROSS, blk, slot % 2) if blk.exists() else None


FIRST, STEADY, LAST = -1, LAG + 1, NBLK - 3
END = NBLK + LAG


def schedule(eng, time):
    for t in range(FIRST, STEADY):
        time(Block(None, t))
    rounds = (LAST + 1 - STEADY) // 2
    with eng.Fori(0, rounds) as i:
        time(Block(i, STEADY))
        time(Block(i, STEADY + 1))
    for t in range(STEADY + 2 * rounds, END + 1):
        time(Block(None, t))


def build(nc, x, ctx_in, cst, w, out):
    f32, f16, bf16 = mybir.dt.float32, mybir.dt.float16, mybir.dt.bfloat16
    ALU, ACT, AX = mybir.AluOpType, mybir.ActivationFunctionType, mybir.AxisListType
    st = ExitStack()

    def sb(name, shape, dt=f32):
        return st.enter_context(nc.sbuf_tensor(name, shape, dt))

    def sem(name):
        return st.enter_context(nc.semaphore(name))

    def two(name):
        return [sem(f"{name}_self"), sem(f"{name}_cross")]

    with st:
        consts = sb("consts", [P, C_END])
        ident = consts[:, C_ID:C_ONES]
        head_mask = consts[:, C_HEAD:C_REV]
        rev_idx = consts[:, C_REV:C_END]
        cbf = sb("consts_bf16", [P, C_HEAD], bf16)
        ident_bf, ones_bf = cbf[:, C_ID:C_ONES], cbf[:, C_ONES:C_MKEY]
        mask_key, mask_qry = cbf[:, C_MKEY:C_MQRY], cbf[:, C_MQRY:C_NEG]
        neg_delta, delta = cbf[:, C_NEG:C_DELTA], cbf[:, C_DELTA:C_HEAD]
        wq = [sb(f"wq{a}", [P, D]) for a in range(2)]
        wk = [sb(f"wk{a}", [P, D]) for a in range(2)]
        wv = [sb(f"wv{a}", [P, D]) for a in range(2)]
        wo = [sb(f"wo{a}", [P, D]) for a in range(2)]
        bq = [sb(f"bq{a}", [P, 1]) for a in range(2)]
        bk = [sb(f"bk{a}", [P, 1]) for a in range(2)]
        bv = [sb(f"bv{a}", [P, D]) for a in range(2)]
        bo = [sb(f"bo{a}", [P, D]) for a in range(2)]
        ln_g = [sb(f"ln_g{a}", [P, D]) for a in range(3)]
        ln_b = [sb(f"ln_b{a}", [P, D]) for a in range(3)]
        ln_gc = [sb(f"ln_gc{a}", [P, 1]) for a in range(2)]
        ln_bc = [sb(f"ln_bc{a}", [P, 1]) for a in range(2)]
        b1_bo = sb("b1_bo", [P, D])
        rw = sb("rw", [P, E])
        rb = sb("rb", [P, E])
        w1 = sb("w1", [P, E, FF])
        w2 = sb("w2", [P, E, FC, D])
        b1_rows = sb("b1_rows", [E * FC, P])
        b1 = sb("b1", [P, E * FC])
        b2 = sb("b2", [E, D])

        tok_in = [[sb(f"tok_in{a}{p}", [P, PAIRS, D]) for p in range(2)] for a in range(2)]
        x_bo = [sb(f"x_bo{p}", [P, PAIRS, D]) for p in range(2)]
        inT = [[sb(f"inT{a}{p}", [P, BT]) for p in range(2)] for a in range(2)]
        x1T = [sb(f"x1T{p}", [P, BT]) for p in range(2)]
        x1_bo = sb("x1_bo", [P, TILES, D])
        x2 = sb("x2", [P, TILES, D])
        x2T = sb("x2T", [P, TOK])
        q_hl = [sb(f"q_hl{a}", [P, 2, BT], f16) for a in range(2)]
        k_hl = [sb(f"k_hl{a}", [P, 2, BT], f16) for a in range(2)]
        q_st = [[sb(f"q_st{a}{p}", [P, G, BT], f16) for p in range(2)] for a in range(2)]
        k_st = [sb(f"k_st{a}", [P, G, BT], f16) for a in range(2)]
        k_all = sb("k_all", [P, 4, G * J * BT], f16)
        k_one = [[k_all[:, 2 * a + p, :].rearrange("p (g j t) -> p g j t", g=G, j=J) for p in range(2)] for a in range(2)]
        v_one = [[sb(f"v_one{a}{p}", [P, PAIRS, 2, H, HD + 1]) for p in range(2)] for a in range(2)]
        row_max = [sb(f"row_max{p}", [P, H], bf16) for p in range(2)]
        max_diag = [sb(f"max_diag{p}", [P, HP, S, 2], bf16) for p in range(2)]
        probT = [sb(f"probT{p}", [P, H, S]) for p in range(2)]
        rden = [sb(f"rden{p}", [P, HP, 2]) for p in range(2)]
        o_n = [sb(f"o_n{p}", [P, 2, 2, HP, HD]) for p in range(2)]
        oT = [sb(f"oT{p}", [P, P]) for p in range(2)]
        res = [sb(f"res{p}", [P, D]) for p in range(2)]
        stats = [sb(f"stats{p}", [P, 6]) for p in range(2)]
        mv = [sb(f"mv{p}", [P, 2]) for p in range(2)]
        rstd = [sb(f"rstd{p}", [P, 1]) for p in range(2)]
        veps = [sb(f"veps{p}", [P, 1]) for p in range(2)]
        carrier = sb("carrier", [P, 1])
        eps = sb("eps", [P, MT])
        minus_half = sb("minus_half", [P, MT])
        yn = [sb(f"yn{p}", [P, D]) for p in range(2)]
        yg = [sb(f"yg{p}", [P, D]) for p in range(2)]

        lg = sb("lg", [P, TILES, E])
        prob = sb("prob", [P, TILES, E])
        tmp = sb("tmp", [P, TILES, E])
        oh1 = sb("oh1", [P, TILES, E])
        oh2 = sb("oh2", [P, TILES, E])
        comb = sb("comb", [P, TILES, E])
        t1 = sb("t1", [P, TILES])
        m1 = sb("m1", [P, TILES])
        m2 = sb("m2", [P, TILES])
        cw1 = sb("cw1", [P, TILES])
        cw2 = sb("cw2", [P, TILES])
        combT = k_all[0:E, 2:4, :].rearrange("p a n -> p (a n)").bitcast(f32)
        hid = [k_all[:, p, :].bitcast(f32).rearrange("p (c t) -> p c t", c=FC) for p in range(2)]
        acc = [sb(f"acc{p}", [P, MT, D]) for p in range(2)]
        fst = sb("fst", [P, MT, 6])
        fmv = sb("fmv", [P, MT, 2])
        frs = sb("frs", [P, MT])
        fin = [sb(f"fin{p}", [P, MT, D]) for p in range(2)]

        bank = st.enter_context(nc.psum_tensor("bank", [P, 8, 512], f32))
        S_B, T_B, O_B, TURN, ROW, QK = 0, 2, 4, 5, 6, 7

        q_scr = [[nc.dram_tensor(f"q_scr{a}{p}", [2, P, BT], f16).ap() for p in range(2)] for a in range(2)]
        k_scr = [[nc.dram_tensor(f"k_scr{a}{p}", [2, P, BT], f16).ap() for p in range(2)] for a in range(2)]

        w_in = sem("weights_in")
        moe_in = sem("moe_weights_in")
        cbf_ready = sem("consts_bf16_ready")
        zeroed = sem("v_one_set")
        tok_landed = [[sem(f"tok_landed{a}{p}") for p in range(2)] for a in range(2)]
        xbo_ready = sem("x_bo_ready")
        inT_ready, inT_done = two("inT_ready"), two("inT_done")
        q_ready, k_ready = two("q_ready"), two("k_ready")
        q_hi, k_hi, q_lo, k_lo = two("q_hi"), two("k_hi"), two("q_lo"), two("k_lo")
        q_out, k_out = two("q_out"), two("k_out")
        q_back = [[sem(f"q_back{a}{p}") for p in range(2)] for a in range(2)]
        k_back = two("k_back")
        k_one_ready = two("k_one_ready")
        v_ready, v_done = two("v_ready"), two("v_done")
        s_ready, max_done, diag_ready = two("s_ready"), two("max_done"), two("diag_ready")
        st_ready, exp_done = two("st_ready"), two("exp_done")
        pv_ready, rden_done, on_ready = two("pv_ready"), two("rden_done"), two("on_ready")
        ot_ready, ot_done = two("ot_ready"), two("ot_done")
        wo_ready, res_done = two("wo_ready"), two("res_done")
        ve_done = two("veps_done")
        st_done, mv_done, rs_done, yn_ready = two("stats_done"), two("mv_done"), two("rstd_done"), two("yn_ready")
        yT_ready, yT_done = two("yT_ready"), two("yT_done")
        yg_done, x_done = two("yg_done"), two("x_done")
        lg_ready, dve_step, act_step = sem("lg_ready"), sem("dve_step"), sem("act_step")
        comb_ready, ct_ready, ct_done = sem("comb_ready"), sem("ct_ready"), sem("ct_done")
        b1_ready, b1_done = sem("b1_ready"), sem("b1_done")
        h_ready, h_done = sem("h_ready"), sem("h_done")
        y_ready, y_done = sem("y_ready"), sem("y_done")
        b2_ready, b2_done = sem("b2_ready"), sem("b2_done")
        f_step, f_rstd, f_veps, f_norm, f_gain, f_ready = sem("f_step"), sem("f_rstd"), sem("f_veps"), sem("f_norm"), sem("f_gain"), sem("f_ready")
        f_out = [sem("f_out0"), sem("f_out1")]

        blk = st.enter_context(nc.Block())
        N_W = [0]

        def prev(now, slot):
            return unit_at(now, slot - 1)

        def row(v):
            return v.rearrange("(a n) -> a n", a=1)

        @blk.sync
        def _(sp):
            def wait(s, v):
                if not isinstance(v, int):
                    sp.compute_val(v)
                settle(sp, w_in, 16 * N_W[0], s, v)

            def load_tokens(a, b):
                src = (x, ctx_in)[a]
                if not b.exists():
                    return
                if b.i is not None or b.off >= 2:
                    wait(inT_ready[a], b.back(2).times(1, 1))
                    if a == SELF:
                        wait(xbo_ready, b.back(2).times(1, 1))
                n = b.times(BT)
                rows = src[n:n + BT, :] if b.i is None else src[bass.ds(n, BT), :]
                sp.dma_start(tok_in[a][b.par][:, :, :], rows.rearrange("(t p) d -> p t d", p=P)).then_inc(
                    tok_landed[a][b.par], 16)

            def send(a, b, hi, lo, hl, scr, gone):
                wait(hi[a], b.times(1, 1))
                wait(lo[a], b.times(1, 1))
                sp.dma_start(scr[a][b.par].rearrange("s p t -> p s t"), hl[a][:, :, :]).then_inc(gone[a], 16)

            def fetch_q(a, b):
                if b.i is not None:
                    sp.compute_val(b.times(16, 16))
                    sp.compute_val(b.back(2).times(2, 2))
                wait(q_out[a], b.times(16, 16))
                if b.i is not None or b.off >= 2:
                    wait(st_ready[a], b.back(2).times(2, 2))
                for s in range(2):
                    for c in range(2):
                        r = 2 * s + c
                        sp.dma_start(q_st[a][b.par][32 * r:32 * r + 32, :, :],
                                     q_scr[a][b.par][s].rearrange("(g p) t -> p g t", g=G)).then_inc(
                                         q_back[a][b.par], 16)

            def fetch_k(a, b):
                if b.i is not None:
                    sp.compute_val(b.times(16, 16))
                    sp.compute_val(b.back(1).times(1, 1))
                wait(k_out[a], b.times(16, 16))
                if b.i is not None or b.off >= 1:
                    wait(k_one_ready[a], b.back(1).times(1, 1))
                for s in range(2):
                    for c in range(2):
                        r = s + 2 * c
                        sp.dma_start(k_st[a][32 * r:32 * r + 32, :, :],
                                     k_scr[a][b.par][s].rearrange("(g p) t -> p g t", g=G)).then_inc(k_back[a], 16)

            def time(now):
                sa, ca = now.back(-1), now.back(1)
                if now.i is not None or now.off >= 0:
                    load_tokens(SELF, now.back(-2))
                    load_tokens(CROSS, now.back(-1))
                if sa.exists():
                    send(SELF, sa, q_hi, q_lo, q_hl, q_scr, q_out)
                    send(SELF, sa, k_hi, k_lo, k_hl, k_scr, k_out)
                    fetch_q(SELF, sa)
                    fetch_k(SELF, sa)
                if ca.exists():
                    send(CROSS, ca, q_hi, q_lo, q_hl, q_scr, q_out)
                    fetch_q(CROSS, ca)
                    send(CROSS, ca, k_hi, k_lo, k_hl, k_scr, k_out)
                    fetch_k(CROSS, ca)

            def load(dst, src, done=w_in):
                sp.dma_start(dst, src).then_inc(done, 16)
                N_W[0] += done is w_in

            load_tokens(SELF, Block(None, 0))
            load(consts[:, :], cst)
            for a, k in enumerate(("sa", "ca")):
                load(wq[a][:, :], w[f"{k}_wq"])
                load(wk[a][:, :], w[f"{k}_wk"])
                load(wv[a][:, :], w[f"{k}_wv"])
                wop = w[f"{k}_wo"].rearrange("(p h d) n -> h p d n", h=2, d=HD)
                for h in range(2):
                    load(wo[a][64 * h:64 * h + 64, :], wop[h])
                load(bq[a][:, :], w[f"{k}_bq"].rearrange("(p a) -> p a", a=1))
                load(bk[a][:, :], w[f"{k}_bk"].rearrange("(p a) -> p a", a=1))
                load(bv[a][:, :], w[f"{k}_bv"].partition_broadcast(P))
                load(bo[a][:, :], w[f"{k}_bo"].partition_broadcast(P))
                load(ln_gc[a][:, :], w[f"ln{a + 1}_g"].rearrange("(p a) -> p a", a=1))
                load(ln_bc[a][:, :], w[f"ln{a + 1}_b"].rearrange("(p a) -> p a", a=1))
                if a == SELF:
                    load_tokens(SELF, Block(None, 1))
                    load_tokens(CROSS, Block(None, 0))
            for a in range(3):
                load(ln_g[a][:, :], w[f"ln{a + 1}_g"].partition_broadcast(P))
                load(ln_b[a][:, :], w[f"ln{a + 1}_b"].partition_broadcast(P))
            load(rw[:, :], w["router_w"])
            load(rb[:, :], w["router_b"].partition_broadcast(P))
            load(w1[:, :, :], w["e_w1"].rearrange("e d f -> d e f"), moe_in)
            load(w2[:, :, :, :], w["e_w2"].rearrange("e (c f) d -> f e c d", c=FC), moe_in)
            load(b1_rows[:, :], w["e_b1"].rearrange("e (c f) -> (e c) f", c=FC), moe_in)
            load(b2[:, :], w["e_b2"], moe_in)
            schedule(sp, time)

            def put(n, buf, rows):
                wait(f_ready, n)
                sp.dma_start(rows.rearrange("(t p) d -> p t d", p=P), fin[buf][:, :, :]).then_inc(f_out[buf], 16)

            with sp.Fori(0, ROUNDS // 2) as i:
                for u in range(2):
                    put(i * 2 + (u + 1), u, out[bass.ds(i * (2 * MB) + u * MB, MB), :])
            for u in range(2):
                sp.wait_ge(f_out[u], 16 * (ROUNDS // 2))

        @blk.gpsimd
        def _(pool):
            for a in range(2):
                for p in range(2):
                    pool.memset(v_one[a][p][:, :, :, :, :], 0.0).then_inc(zeroed, 1)
            for p in range(2):
                pool.memset(o_n[p][:, :, :, :, :], 0.0).then_inc(zeroed, 1)
            pool.memset(minus_half[:, :], -0.5).then_inc(zeroed, 1)
            pool.memset(eps[:, :], EPS).then_inc(zeroed, 1)
            pool.wait_ge(zeroed, 8)
            for a in range(2):
                for p in range(2):
                    for b in range(2):
                        pool.memset(v_one[a][p][64 * b:64 * b + 64, :, b, :, HD:HD + 1], 1.0).then_inc(zeroed, 1)
                        pool.wait_ge(zeroed, 8 + 4 * a + 2 * p + b + 1)
            pool.wait_ge(zeroed, 16)
            pool.wait_ge(w_in, 16 * N_W[0])
            pool.tensor_tensor(b1_bo[:, :], ln_b[0][:, :], bo[CROSS][:, :], ALU.add).then_inc(zeroed, 1)
            pool.wait_ge(zeroed, 17)

            def add_bo(b):
                pool.wait_ge(tok_landed[SELF][b.par], b.landed())
                if b.i is not None or b.off >= 2:
                    pool.wait_ge(res_done[SELF], b.back(2).times(2, 2))
                pool.tensor_tensor(x_bo[b.par][:, :, :], tok_in[SELF][b.par][:, :, :],
                                   bo[SELF][:, :].unsqueeze(1).to_broadcast([P, PAIRS, D]), ALU.add).then_inc(xbo_ready, 1)

            def spread(u):
                a, n = u.kind, u.buf
                pool.wait_ge(mv_done[a], u.count())
                pool.tensor_tensor(veps[n][:, :], mv[n][:, 1:2], eps[:, 0:1], ALU.add).then_inc(ve_done[a], 1)
                pool.wait_ge(ve_done[a], u.count())
                pool.tensor_tensor(rstd[n][:, :], veps[n][:, :], minus_half[:, 0:1], ALU.pow).then_inc(rs_done[a], 1)

            def gain(u):
                a = u.kind
                pool.wait_ge(yn_ready[a], u.count())
                pool.tensor_tensor(yg[u.buf][:, :], yn[u.buf][:, :], ln_g[a][:, :], ALU.mult).then_inc(yg_done[a], 1)
                pool.wait_ge(yg_done[a], u.count())
                dst = (x1_bo, x2)[a][:, u.tile(), :]
                off = (b1_bo, ln_b[1])[a]
                pool.tensor_tensor(dst, yg[u.buf][:, :], off[:, :], ALU.add).then_inc(x_done[a], 1)

            def time(now):
                for s in range(4):
                    if s == 0 and now.back(-1).exists():
                        add_bo(now.back(-1))
                    if u := unit_at(now, s - 4):
                        gain(u)
                    if u := unit_at(now, s - 3):
                        spread(u)

            schedule(pool, time)
            with pool.Fori(0, ROUNDS // 2) as i:
                for u in range(2):
                    pool.wait_ge(f_step, i * 4 + (2 * u + 3))
                    pool.tensor_tensor(frs[:, :], fmv[:, :, 1], eps[:, :], ALU.add).then_inc(f_veps, 1)
                    pool.wait_ge(f_veps, i * 2 + (u + 1))
                    pool.tensor_tensor(frs[:, :], frs[:, :], minus_half[:, :], ALU.pow).then_inc(f_rstd, 1)
                    pool.wait_ge(f_norm, i * 2 + (u + 1))
                    pool.wait_ge(f_out[u], i * 16)
                    pool.tensor_tensor(fin[u][:, :, :], acc[u][:, :, :],
                                       ln_g[2][:, :].unsqueeze(1).to_broadcast([P, MT, D]), ALU.mult).then_inc(f_gain, 1)
                    pool.wait_ge(f_gain, i * 2 + (u + 1))
                    pool.tensor_tensor(fin[u][:, :, :], fin[u][:, :, :],
                                       ln_b[2][:, :].unsqueeze(1).to_broadcast([P, MT, D]), ALU.add).then_inc(f_ready, 1)

        @blk.scalar
        def _(act):
            act.wait_ge(w_in, 16 * N_W[0])

            def turned(a, b):
                act.wait_ge(inT_ready[a], b.times(1, 1))
                if b.i is not None or b.off >= 2:
                    act.wait_ge(v_ready[a], b.back(2).times(1, 1))
                act.activation(inT[a][b.par][:, :], bank[:, TURN, 0:BT], ACT.Copy).then_inc(inT_done[a], 1)

            def high(a, b, ready, hi, hl, bias, gone, col):
                act.wait_ge(ready[a], b.times(1, 1))
                if b.i is not None or b.off >= 1:
                    act.wait_ge(gone[a], b.times(16))
                act.activation(hl[a][:, 0, :], bank[:, QK, col:col + BT], ACT.Identity, bias=bias[a][:, :]).then_inc(hi[a], 1)

            def exps(u):
                a = u.kind
                act.wait_ge(st_ready[a], u.count())
                v = before(u)
                if v:
                    act.wait_ge(pv_ready[v.kind], v.count())
                act.activation(probT[u.buf][:, :, :].rearrange("p h q -> p (h q)"),
                               bank[:, T_B:T_B + 2, :].rearrange("p a n -> p (a n)"), ACT.Exp,
                               scale=float(HD) ** -0.5).then_inc(exp_done[a], 1)

            def o_turned(u):
                a = u.kind
                act.wait_ge(ot_ready[a], u.count())
                v = before(u)
                if v:
                    act.wait_ge(wo_ready[v.kind], v.count())
                act.activation(oT[u.buf][:, :], bank[:, TURN, 0:P], ACT.Copy).then_inc(ot_done[a], 1)

            def y_turned(u):
                a = u.kind
                act.wait_ge(yT_ready[a], u.count())
                if a == SELF:
                    dst = x1T[u.blk.par][:, u.col:u.col + P]
                    if u.blk.i is not None or u.blk.off >= 2:
                        act.wait_ge(q_ready[CROSS], u.blk.back(2).times(1, 1))
                else:
                    n = u.blk.times(BT, u.col)
                    dst = x2T[:, n:n + P] if u.blk.i is None else x2T[:, bass.ds(n, P)]
                act.activation(dst, bank[:, TURN, 0:P], ACT.Identity, bias=ln_bc[a][:, :], scale=ln_gc[a][:, :]).then_inc(
                    yT_done[a], 1)

            def before(u):
                if u.kind == SELF:
                    b = u.blk.back(1 + LAG)
                    return Unit(CROSS, b, u.pair) if b.exists() else None
                b = u.blk.back(-LAG)
                return Unit(SELF, b, u.pair) if b.exists() else None

            def time(now):
                sa, ca = now.back(-1), now.back(1)
                for s in range(4):
                    if u := unit_at(now, s - 3):
                        o_turned(u)
                    if u := unit_at(now, s - 1):
                        exps(u)
                    if u := unit_at(now, s - 4):
                        y_turned(u)
                    if s == 0:
                        if sa.exists():
                            turned(SELF, sa)
                        if ca.exists():
                            turned(CROSS, ca)
                    if s == 1 and sa.exists():
                        high(SELF, sa, q_ready, q_hi, q_hl, bq, q_out, 0)
                        high(SELF, sa, k_ready, k_hi, k_hl, bk, k_out, 0)
                    if s == 2 and ca.exists():
                        high(CROSS, ca, q_ready, q_hi, q_hl, bq, q_out, 0)
                    if s == 3 and ca.exists():
                        high(CROSS, ca, k_ready, k_hi, k_hl, bk, k_out, 0)

            schedule(act, time)

            act.wait_ge(dve_step, 3)
            act.activation(tmp[:, :, :], lg[:, :, :], ACT.Exp).then_inc(act_step, 1)
            act.wait_ge(dve_step, 17)
            act.activation(t1[:, :], m2[:, :], ACT.Exp).then_inc(act_step, 1)
            for t in range(ROUNDS):
                act.wait_ge(ct_ready, t + 1)
                act.activation(combT[:, t * MB:(t + 1) * MB], bank[0:E, t % 2, :], ACT.Copy).then_inc(ct_done, 1)

            act.wait_ge(b1_ready, 1)
            act.activation(b1[:, :], bank[:, 4, 0:E * FC], ACT.Copy).then_inc(b1_done, 1)
            act.wait_ge(b1_done, 1)

            def gelus(i, n, first=False):
                for e in range(E):
                    for c in range(FC):
                        k = e * FC + c
                        act.wait_ge(h_ready, i * (E * FC) + (k + 1))
                        if c == 0 and not (first and e < 2):
                            act.wait_ge(y_ready, i * E + (e - 1))
                        act.activation(hid[e % 2][:, c, :], bank[:, c, :], ACT.Gelu,
                                       bias=b1[:, k:k + 1]).then_inc(h_done, 1)
            gelus(0, 0, True)
            with act.Fori(1, ROUNDS) as i:
                gelus(i, 0)

        @blk.vector
        def _(dve):
            dve.wait_ge(w_in, 16 * N_W[0])
            dve.tensor_copy(cbf[:, :], consts[:, 0:C_HEAD]).then_inc(cbf_ready, 1)
            dve.wait_ge(cbf_ready, 1)
            dve.wait_ge(zeroed, 17)

            def low(a, b, hi, lo, hl, bias, gone, col):
                dve.wait_ge(hi[a], b.times(1, 1))
                dve.scalar_tensor_tensor(hl[a][:, 1, :], bank[:, QK, col:col + BT], bias[a][:, :], hl[a][:, 0, :],
                                         ALU.add, ALU.subtract).then_inc(lo[a], 1)

            def masks(a, b):
                dve.wait_ge(k_back[a], b.times(64, 64))
                if b.i is not None or b.off >= 2:
                    dve.wait_ge(st_ready[a], b.back(2).times(2, 2))
                for j in range(J):
                    last = dve.tensor_scalar(k_one[a][b.par][:, :, j, :], k_st[a][:, :, :],
                                             head_mask[:, j:j + 1], None, ALU.mult)
                last.then_inc(k_one_ready[a], 1)

            def v_rows(a, b):
                dve.wait_ge(v_ready[a], b.times(1, 1))
                if b.i is not None or b.off >= 2:
                    dve.wait_ge(pv_ready[a], b.back(2).times(2, 2))
                for h in range(2):
                    r = slice(64 * h, 64 * h + 64)
                    last = dve.tensor_tensor(
                        v_one[a][b.par][r, :, h, :, 0:HD],
                        bank[r, ROW, 0:BT].rearrange("p (t h d) -> p t h d", t=PAIRS, h=H),
                        bv[a][r, :].rearrange("p (h d) -> p h d", h=H).unsqueeze(1).to_broadcast([64, PAIRS, H, HD]),
                        ALU.add)
                last.then_inc(v_done[a], 1)

            def maxima(u):
                a = u.kind
                dve.wait_ge(s_ready[a], u.count())
                dve.reduce_max(row_max[u.buf][:, :],
                               bank[:, S_B:S_B + 2, :].rearrange("p a (h k) -> p (a h) k", k=S), AX.X).then_inc(max_done[a], 1)
                dve.wait_ge(max_done[a], u.count())
                m = row_max[u.buf][:, :].rearrange("p (a c) -> p a c", c=2).unsqueeze(2).to_broadcast([P, HP, S, 2])
                dl = neg_delta.rearrange("p (q c) -> p q c", c=2).unsqueeze(1).to_broadcast([P, HP, S, 2])
                dve.tensor_tensor(max_diag[u.buf][:, :, :, :], dl, m, ALU.mult).then_inc(diag_ready[a], 1)

            def outputs(u):
                a = u.kind
                dve.wait_ge(pv_ready[a], u.count())
                o = bank[:, O_B, 0:HP * 36].rearrange("p (a b c d) -> p a b c d", a=HP, b=2, c=2)
                for h in range(2):
                    r = slice(64 * h, 64 * h + 64)
                    last = dve.reciprocal(rden[u.buf][r, :, :], o[r, :, :, h, HD])
                last.then_inc(rden_done[a], 1)
                dve.wait_ge(rden_done[a], u.count())
                for h in range(2):
                    r = slice(64 * h, 64 * h + 64)
                    last = dve.tensor_tensor(o_n[u.buf][r, :, h, :, :].rearrange("p b a d -> p a b d"), o[r, :, :, h, 0:HD],
                                             rden[u.buf][r, :, :].unsqueeze(3).to_broadcast([64, HP, 2, HD]), ALU.mult)
                last.then_inc(on_ready[a], 1)

            def norm(u):
                a, n = u.kind, u.buf
                dve.wait_ge(wo_ready[a], u.count())
                if a == SELF:
                    dve.wait_ge(xbo_ready, u.blk.times(1, 1))
                    r = x_bo[u.blk.par][:, u.pair, :]
                else:
                    dve.wait_ge(x_done[SELF], u.count())
                    r = x1_bo[:, u.tile(), :]
                dve.tensor_tensor(res[n][:, :], bank[:, ROW, 0:D], r, ALU.add).then_inc(res_done[a], 1)
                dve.wait_ge(res_done[a], u.count())
                dve.bn_stats(stats[n][:, :], res[n][:, :]).then_inc(st_done[a], 1)
                dve.wait_ge(st_done[a], u.count())
                dve.tensor_copy(carrier[:, :], consts[:, 0:1])
                dve.bn_aggr(mv[n][:, :], stats[n][:, :]).then_inc(mv_done[a], 1)
                dve.wait_ge(rs_done[a], u.count())
                if u.kind == SELF:
                    v = Unit(CROSS, u.blk.back(1 + LAG), u.pair)
                else:
                    v = Unit(SELF, u.blk.back(-LAG), u.pair)
                if v.blk.exists():
                    dve.wait_ge(yT_ready[v.kind], v.count())
                    dve.wait_ge(yg_done[v.kind], v.count())
                dve.tensor_scalar(yn[n][:, :], res[n][:, :], mv[n][:, 0:1], rstd[n][:, :], ALU.subtract,
                                  ALU.mult).then_inc(yn_ready[a], 1)

            def time(now):
                sa, ca = now.back(-1), now.back(1)
                for s in range(4):
                    if u := unit_at(now, s):
                        maxima(u)
                    if s == 1 and sa.exists():
                        low(SELF, sa, q_hi, q_lo, q_hl, bq, q_out, 0)
                        low(SELF, sa, k_hi, k_lo, k_hl, bk, k_out, 0)
                    if s == 2 and ca.exists():
                        low(CROSS, ca, q_hi, q_lo, q_hl, bq, q_out, 0)
                    if s == 3 and ca.exists():
                        low(CROSS, ca, k_hi, k_lo, k_hl, bk, k_out, 0)
                    if u := unit_at(now, s - 2):
                        outputs(u)
                    if u := unit_at(now, s - 3):
                        norm(u)
                    if s == 2 and sa.exists():
                        v_rows(SELF, sa)
                    if s == 3 and ca.exists():
                        v_rows(CROSS, ca)
                    if s == 3 and sa.exists():
                        masks(SELF, sa)
                    if s == 1 and ca.back(1).exists():
                        masks(CROSS, ca.back(1))

            schedule(dve, time)

            n = [0]

            def step(ins):
                n[0] += 1
                ins.then_inc(dve_step, 1)
                dve.wait_ge(dve_step, n[0])

            def wide(v):
                return v[:, :].unsqueeze(2).to_broadcast([P, TILES, E])

            def first_max(m, onehot):
                step(dve.reduce_max(m[:, :], prob[:, :, :], AX.X))
                step(dve.tensor_tensor(tmp[:, :, :], prob[:, :, :], wide(m), ALU.is_equal))
                step(dve.tensor_tensor(tmp[:, :, :], tmp[:, :, :],
                                       rev_idx.unsqueeze(1).to_broadcast([P, TILES, E]), ALU.mult))
                step(dve.reduce_max(t1[:, :], tmp[:, :, :], AX.X))
                step(dve.tensor_tensor(onehot[:, :, :], tmp[:, :, :], wide(t1), ALU.is_equal))

            dve.wait_ge(lg_ready, 1)
            step(dve.tensor_tensor(lg[:, :, :], bank[:, QK, 0:TILES * E].rearrange("p (t e) -> p t e", e=E),
                                   rb[:, :].unsqueeze(1).to_broadcast([P, TILES, E]), ALU.add))
            step(dve.reduce_max(t1[:, :], lg[:, :, :], AX.X))
            step(dve.tensor_tensor(lg[:, :, :], lg[:, :, :], wide(t1), ALU.subtract))
            dve.wait_ge(act_step, 1)
            step(dve.reduce_sum(t1[:, :], tmp[:, :, :], AX.X))
            step(dve.reciprocal(t1[:, :], t1[:, :]))
            step(dve.tensor_tensor(prob[:, :, :], tmp[:, :, :], wide(t1), ALU.mult))
            first_max(m1, oh1)
            step(dve.scalar_tensor_tensor(prob[:, :, :].rearrange("p t e -> p (t e)"),
                                          oh1[:, :, :].rearrange("p t e -> p (t e)"), -2.0,
                                          prob[:, :, :].rearrange("p t e -> p (t e)"), ALU.mult, ALU.add))
            step(dve.reduce_max(m2[:, :], prob[:, :, :], AX.X))
            step(dve.tensor_tensor(tmp[:, :, :], prob[:, :, :], wide(m2), ALU.is_equal))
            step(dve.tensor_tensor(tmp[:, :, :], tmp[:, :, :],
                                   rev_idx.unsqueeze(1).to_broadcast([P, TILES, E]), ALU.mult))
            step(dve.reduce_max(t1[:, :], tmp[:, :, :], AX.X))
            dve.tensor_tensor(m2[:, :], m2[:, :], m1[:, :], ALU.subtract).then_inc(f_step, 1)
            dve.wait_ge(f_step, 1)
            step(dve.tensor_tensor(oh2[:, :, :], tmp[:, :, :], wide(t1), ALU.is_equal))
            assert n[0] == 17, n
            dve.wait_ge(act_step, 2)
            step(dve.tensor_scalar(cw1[:, :], t1[:, :], 1.0, None, ALU.add))
            step(dve.reciprocal(cw1[:, :], cw1[:, :]))
            step(dve.tensor_tensor(cw2[:, :], t1[:, :], cw1[:, :], ALU.mult))
            step(dve.tensor_tensor(oh1[:, :, :], oh1[:, :, :], wide(cw1), ALU.mult))
            step(dve.tensor_tensor(oh2[:, :, :], oh2[:, :, :], wide(cw2), ALU.mult))
            dve.tensor_tensor(comb[:, :, :], oh1[:, :, :], oh2[:, :, :], ALU.add).then_inc(comb_ready, 1)
            dve.wait_ge(x_done[CROSS], TILES)
            for r in range(ROUNDS):
                dve.wait_ge(b2_ready, r + 1)
                x2r = x2[:, r * MT:(r + 1) * MT, :]
                dve.tensor_tensor(x2r, x2r, bank[:, 2 + r % 2, :].rearrange("p (t d) -> p t d", t=MT),
                                  ALU.add).then_inc(b2_done, 1)
            dve.wait_ge(b2_done, ROUNDS)

            F0 = 1

            def combine(i, u, start):
                a = acc[u]
                if not start:
                    dve.wait_ge(f_gain, i * 2 + (u - 1))
                for e in range(E):
                    dve.wait_ge(y_ready, i * (2 * E) + (u * E + e + 1))
                    for t in range(MT):
                        tile = u * MT + t
                        c = comb[:, tile, e:e + 1] if start else comb[:, bass.ds(i * (2 * MT) + tile, 1), e]
                        add = a[:, t, :] if e else x2[:, tile, :] if start else x2[:, i * (2 * MT) + tile, :]
                        last = dve.scalar_tensor_tensor(a[:, t, :], bank[:, 4 + e % 2, t * D:(t + 1) * D], c, add,
                                                        ALU.mult, ALU.add)
                    last.then_inc(y_done, 1)
                    dve.wait_ge(y_done, i * (2 * E) + (u * E + e + 1))
                base = F0 + 2 * u
                for t in range(MT):
                    last = dve.bn_stats(fst[:, t, :], a[:, t, :])
                last.then_inc(f_step, 1)
                dve.wait_ge(f_step, i * 4 + (base + 1))
                dve.tensor_copy(carrier[:, :], consts[:, 0:1])
                for t in range(MT):
                    last = dve.bn_aggr(fmv[:, t, :], fst[:, t, :])
                last.then_inc(f_step, 1)
                dve.wait_ge(f_step, i * 4 + (base + 2))
                dve.wait_ge(f_rstd, i * 2 + (u + 1))
                for t in range(MT):
                    last = dve.tensor_scalar(a[:, t, :], a[:, t, :], fmv[:, t, 0:1], frs[:, t:t + 1], ALU.subtract, ALU.mult)
                last.then_inc(f_norm, 1)

            for u in range(2):
                combine(0, u, True)
            with dve.Fori(1, ROUNDS // 2) as i:
                for u in range(2):
                    combine(i, u, False)

        @blk.tensor
        def _(pe):
            pe.wait_ge(cbf_ready, 1)

            def free(users):
                for s, v in users:
                    pe.wait_ge(s, v)

            def turn_free(now, s, part):
                order = [(q, k) for q in range(s - 8, s + 1) for k in ("o", "y", "x", "c")]
                order = order[:order.index((s, part))]
                for q, k in reversed(order):
                    t = now.back(-(q // 4))
                    if k == "o" and (u := unit_at(now, q - 3)):
                        return pe.wait_ge(ot_done[u.kind], u.count())
                    if k == "y" and (u := unit_at(now, q - 4)):
                        return pe.wait_ge(yT_done[u.kind], u.count())
                    if k == "x" and q % 4 == 0 and t.back(-1).exists():
                        return pe.wait_ge(inT_done[SELF], t.back(-1).times(1, 1))
                    if k == "c" and q % 4 == 0 and t.back(1).exists():
                        return pe.wait_ge(inT_done[CROSS], t.back(1).times(1, 1))

            def row_free(now, s, part):
                order = [(q, k) for q in range(s - 8, s + 1) for k in ("wo", "v")]
                order = order[:order.index((s, part))]
                for q, k in reversed(order):
                    t = now.back(-(q // 4))
                    if k == "wo" and (u := unit_at(now, q - 3)):
                        return pe.wait_ge(res_done[u.kind], u.count())
                    if k == "v" and q % 4 == 2 and t.back(-1).exists():
                        return pe.wait_ge(v_done[SELF], t.back(-1).times(1, 1))
                    if k == "v" and q % 4 == 3 and t.back(1).exists():
                        return pe.wait_ge(v_done[CROSS], t.back(1).times(1, 1))

            def qk_free(now, s, part):
                order = [(q, k) for q in range(s - 8, s + 1) for k in ("q", "k")]
                order = order[:order.index((s, part))]
                for q, k in reversed(order):
                    t = now.back(-(q // 4))
                    sa, ca = t.back(-1), t.back(1)
                    if q % 4 == 1 and sa.exists():
                        return pe.wait_ge((q_lo, k_lo)[k == "k"][SELF], sa.times(1, 1))
                    if q % 4 == 2 and k == "q" and ca.exists():
                        return pe.wait_ge(q_lo[CROSS], ca.times(1, 1))
                    if q % 4 == 3 and k == "k" and ca.exists():
                        return pe.wait_ge(k_lo[CROSS], ca.times(1, 1))

            def turn_in(now, s, a, b):
                pe.wait_ge(tok_landed[a][b.par], b.landed())
                turn_free(now, s, "xc"[a])
                for t in range(PAIRS):
                    last = pe.transpose(bank[:, TURN, t * P:(t + 1) * P], tok_in[a][b.par][:, t, :], ident)
                last.then_inc(inT_ready[a], 1)

            def project(now, s, part, wt, src, ready, a):
                qk_free(now, s, part)
                pe.matmul(bank[:, QK, 0:BT], wt[a][:, :], src[:, :], start=True, stop=True).then_inc(ready[a], 1)

            def v_proj(now, s, a, b):
                row_free(now, s, "v")
                for t in range(PAIRS):
                    last = pe.matmul(bank[:, ROW, t * P:(t + 1) * P], inT[a][b.par][:, t * P:(t + 1) * P], wv[a][:, :],
                                     start=True, stop=True)
                last.then_inc(v_ready[a], 1)

            def scores(u, v):
                a, b = u.kind, u.blk
                pe.wait_ge(q_back[a][b.par], b.landed(64))
                pe.wait_ge(k_one_ready[a], b.times(1, 1))
                if v:
                    pe.wait_ge(max_done[v.kind], v.count())
                q, k = q_st[a][b.par], k_one[a][b.par]
                for n in range(2):
                    if a == SELF:
                        pe.matmul(bank[:, S_B + n, :], ident_bf, mask_key.unsqueeze(1).to_broadcast([P, H // 2, S]),
                                  start=True, stop=True)
                    for gi in range(2):
                        for h in range(2):
                            c = u.col + 64 * h
                            last = pe.matmul(bank[64 * h:64 * h + 64, S_B + n, 256 * gi:256 * gi + 256],
                                             q[:, 2 * n + gi, c:c + 64], k[:, 2 * n + gi, :, c:c + 64],
                                             start=a == CROSS and gi == 0, stop=True, skip_group_check=True)
                last.then_inc(s_ready[a], 1)

            def scores_T(u, v):
                a, b = u.kind, u.blk
                pe.wait_ge(diag_ready[a], u.count())
                if v:
                    pe.wait_ge(exp_done[v.kind], v.count())
                q, k = q_st[a][b.par], k_one[a][b.par]
                for n in range(2):
                    pe.matmul(bank[:, T_B + n, :], ones_bf,
                              max_diag[u.buf][:, 4 * n:4 * n + 4, :, :].rearrange("p a q c -> p a c q"),
                              start=True, stop=True)
                    if a == SELF:
                        pe.matmul(bank[:, T_B + n, :], mask_qry, delta.unsqueeze(1).to_broadcast([P, H // 2, S]),
                                  start=False, stop=True, skip_group_check=True)
                    for hh in range(H // 2):
                        g, j = divmod(8 * n + hh, J)
                        for h in range(2):
                            c = u.col + 64 * h
                            last = pe.matmul(bank[64 * h:64 * h + 64, T_B + n, 64 * hh:64 * hh + 64],
                                             k[:, g, j, c:c + 64], q[:, g, c:c + 64],
                                             start=False, stop=True, skip_group_check=True)
                last.then_inc(st_ready[a], 1)

            def weigh(u, v):
                a, b = u.kind, u.blk
                pe.wait_ge(exp_done[a], u.count())
                pe.wait_ge(v_done[a], b.times(1, 1))
                if v:
                    pe.wait_ge(on_ready[v.kind], v.count())
                for p in range(HP):
                    last = pe.matmul(bank[:, O_B, 36 * p:36 * p + 36],
                                     probT[u.buf][:, 2 * p:2 * p + 2, :].rearrange("p h q -> p (h q)"),
                                     v_one[a][b.par][:, u.pair, :, 2 * p:2 * p + 2, :].rearrange("p b h d -> p b (h d)"),
                                     start=True, stop=True)
                last.then_inc(pv_ready[a], 1)

            def turn_o(now, s, u):
                turn_free(now, s, "o")
                pe.wait_ge(on_ready[u.kind], u.count())
                for b in range(2):
                    last = pe.matmul(bank[:, TURN, 64 * b:64 * b + 64],
                                     o_n[u.buf][:, b, :, :, :].rearrange("p c a d -> p (c a d)"),
                                     consts[:, C_DELTA:C_HEAD], start=True, stop=True)
                last.then_inc(ot_ready[u.kind], 1)

            def out_proj(now, s, u):
                pe.wait_ge(ot_done[u.kind], u.count())
                row_free(now, s, "wo")
                pe.matmul(bank[:, ROW, 0:D], oT[u.buf][:, :], wo[u.kind][:, :], start=True, stop=True).then_inc(
                    wo_ready[u.kind], 1)

            def turn_y(now, s, u):
                pe.wait_ge(yn_ready[u.kind], u.count())
                turn_free(now, s, "y")
                pe.transpose(bank[:, TURN, 0:P], yn[u.buf][:, :], ident).then_inc(yT_ready[u.kind], 1)

            def time(now):
                sa, ca = now.back(-1), now.back(1)
                for s in range(4):
                    if u := unit_at(now, s - 3):
                        turn_o(now, s, u)
                    if u := unit_at(now, s):
                        scores(u, prev(now, s))
                    if s == 1 and sa.exists():
                        pe.wait_ge(inT_done[SELF], sa.times(1, 1))
                        project(now, s, "q", wq, inT[SELF][sa.par], q_ready, SELF)
                    if s == 2 and ca.exists():
                        pe.wait_ge(yT_done[SELF], ca.times(2, 2))
                        project(now, s, "q", wq, x1T[ca.par], q_ready, CROSS)
                    if s == 3 and ca.exists():
                        pe.wait_ge(inT_done[CROSS], ca.times(1, 1))
                        project(now, s, "k", wk, inT[CROSS][ca.par], k_ready, CROSS)
                    if u := unit_at(now, s - 1):
                        scores_T(u, unit_at(now, s - 2))
                    if u := unit_at(now, s - 3):
                        out_proj(now, s, u)
                    if u := unit_at(now, s - 4):
                        turn_y(now, s, u)
                    if s == 0 and sa.exists():
                        turn_in(now, s, SELF, sa)
                    if s == 1 and sa.exists():
                        project(now, s, "k", wk, inT[SELF][sa.par], k_ready, SELF)
                    if u := unit_at(now, s - 2):
                        weigh(u, unit_at(now, s - 3))
                    if s == 0 and ca.exists():
                        turn_in(now, s, CROSS, ca)
                    if s == 2 and sa.exists():
                        v_proj(now, s, SELF, sa)
                    if s == 3 and ca.exists():
                        v_proj(now, s, CROSS, ca)

            schedule(pe, time)

            def out_bias(r):
                pe.wait_ge(ct_done, r + 1)
                if r >= 2:
                    pe.wait_ge(b2_done, r - 1)
                for t in range(MT):
                    k = r * MT + t
                    last = pe.matmul(bank[:, 2 + r % 2, t * D:(t + 1) * D], combT[:, k * P:(k + 1) * P], b2[:, :],
                                     start=True, stop=True)
                last.then_inc(b2_ready, 1)

            pe.wait_ge(yT_done[CROSS], TILES)
            for t in range(TILES):
                last = pe.matmul(bank[:, QK, t * E:(t + 1) * E], x2T[:, t * P:(t + 1) * P], rw[:, :], start=True, stop=True)
            last.then_inc(lg_ready, 1)
            pe.wait_ge(moe_in, 64)
            pe.transpose(bank[:, 4, 0:E * FC], b1_rows[:, :], ident[0:E * FC, 0:E * FC]).then_inc(b1_ready, 1)
            pe.wait_ge(comb_ready, 1)
            for r in range(ROUNDS):
                if r >= 2:
                    pe.wait_ge(ct_done, r - 1)
                for t in range(MT):
                    last = pe.transpose(bank[0:E, r % 2, t * P:(t + 1) * P], comb[:, r * MT + t, :], ident)
                last.then_inc(ct_ready, 1)
                if r >= 1:
                    out_bias(r - 1)
            out_bias(ROUNDS - 1)

            def up(i, e, first):
                for c in range(FC):
                    if not (first and e == 0):
                        pe.wait_ge(h_done, i * (E * FC) + ((e - 1) * FC + c + 1))
                    src = x2T[:, 0:MB] if first else x2T[:, bass.ds(i * MB, MB)]
                    pe.matmul(bank[:, c, :], w1[:, e, c * P:(c + 1) * P], src, start=True, stop=True).then_inc(h_ready, 1)

            def down(i, e, first):
                pe.wait_ge(h_done, i * (E * FC) + (e * FC + FC))
                if not (first and e < 2):
                    pe.wait_ge(y_done, i * E + (e - 1))
                for t in range(MT):
                    for c in range(FC):
                        last = pe.matmul(bank[:, 4 + e % 2, t * D:(t + 1) * D], hid[e % 2][:, c, t * P:(t + 1) * P],
                                         w2[:, e, c, :], start=c == 0, stop=c == FC - 1, skip_group_check=True)
                last.then_inc(y_ready, 1)

            def experts(i, first):
                for e in range(E):
                    up(i, e, first)
                    if e:
                        down(i, e - 1, first)
                down(i, E - 1, first)

            pe.wait_ge(b2_done, ROUNDS)
            pe.wait_ge(b1_done, 1)
            experts(0, True)
            with pe.Fori(1, ROUNDS) as i:
                experts(i, False)


_INS = ['x', 'ctx_1024', 'sa_wq', 'sa_bq', 'sa_wk', 'sa_bk', 'sa_wv', 'sa_bv', 'sa_wo', 'sa_bo', 'ca_wq', 'ca_bq', 'ca_wk',
        'ca_bk', 'ca_wv', 'ca_bv', 'ca_wo', 'ca_bo', 'ln1_g', 'ln1_b', 'ln2_g', 'ln2_b', 'ln3_g', 'ln3_b', 'router_w',
        'router_b', 'e_w1', 'e_b1', 'e_w2', 'e_b2']


def kernel(**inputs):
    import numpy as _np
    import concourse.bacc as _bacc
    from concourse import mybir as _mybir
    from concourse.bass_utils import run_bass_kernel_spmd as _run

    nc = _bacc.Bacc("TRN2", target_bir_lowering=False, num_devices=1)
    arrays, aps = {}, {}

    def give(name, a):
        arrays[f"in_{name}"] = _np.ascontiguousarray(a)
        aps[name] = nc.dram_tensor(f"in_{name}", a.shape, _mybir.dt.from_np(a.dtype), kind="ExternalInput").ap()

    for name in _INS:
        a = _np.asarray(inputs[name if name in ("x", "ctx_1024") else "L0_xattn_" + name])
        give(name, a.reshape(TOK, D) if name in ("x", "ctx_1024") else a)
    give("consts", shape_constants())
    out = nc.dram_tensor("out", (TOK, D), _mybir.dt.float32, kind="ExternalOutput").ap()
    build(nc, aps["x"], aps["ctx_1024"], aps["consts"], aps, out)
    r = _run(nc, [arrays], core_ids=[0])
    return r.results[0]["out"].reshape(B, S, D)
```

```python
import numpy as np
import concourse.bass as bass
from concourse import mybir
from contextlib import ExitStack

B, S, D, H, FF, E = 64, 64, 128, 16, 512, 8
HD = D // H
P = 128
TOK = B * S
TILES = TOK // P
PAIRS = 2
BT = PAIRS * P
NBLK = TOK // BT
G = 4
J = H // G
HP = H // 2
SELF, CROSS = 0, 1
LAG = 2
EPS = 1e-5
MASKED = -1e30
FC = FF // P
MB = 512
MT = MB // P
ROUNDS = TOK // MB
ROUTE_STEPS = 21

C_ID, C_ONES, C_MKEY, C_MQRY, C_NEG, C_DELTA, C_HEAD, C_REV, C_END = np.cumsum(
    [0, P, P, S, P, 2 * S, S, J, E]).tolist()


def shape_constants():
    c = np.zeros((P, C_END), np.float32)
    p = np.arange(P)
    batch, tok = p // S, p % S
    same = batch[:, None] == batch[None, :]
    c[:, C_ID:C_ONES] = np.eye(P)
    c[:, C_ONES:C_MKEY] = same
    c[:, C_MKEY:C_MQRY] = np.where(np.arange(S)[None, :] > tok[:, None], MASKED, 0)
    c[:, C_MQRY:C_NEG] = np.where(same & (tok[None, :] > tok[:, None]), MASKED, 0)
    c[:, C_NEG:C_DELTA] = -np.repeat(tok[:, None] == np.arange(S)[None, :], 2, axis=1).astype(np.float32)
    c[:, C_DELTA:C_HEAD] = tok[:, None] == np.arange(S)[None, :]
    c[:, C_HEAD:C_REV] = (p[:, None] % 32) // HD == np.arange(J)[None, :]
    c[:, C_REV:C_END] = E - np.arange(E)[None, :]
    return c


class Block:

    def __init__(self, i, off, rounds=1):
        self.i, self.off, self.rounds, self.par = i, off, rounds, off % 2

    def back(self, d):
        return Block(self.i, self.off - d, self.rounds)

    def exists(self):
        first, last = (0 <= n < NBLK for n in (self.off, self.off + 2 * (self.rounds - 1)))
        assert first == last
        return first

    def times(self, m, add=0):
        return m * self.off + add if self.i is None else self.i * (2 * m) + (m * self.off + add)

    def landed(self, per=16):
        h = self.off // 2
        return (h + 1) * per if self.i is None else self.i * per + (h + 1) * per


class Expert:

    def __init__(self, i, off, e, rounds):
        self.i, self.off, self.e, self.rounds = i, off, e, rounds

    def exists(self):
        first, last = (0 <= n < ROUNDS for n in (self.off, self.off + self.rounds - 1))
        assert first == last
        return first

    def times(self, m, add=0):
        return m * self.off + add if self.i is None else self.i * m + (m * self.off + add)

    def early(self, n):
        return self.i is None and E * self.off + self.e < n

    def count(self):
        return self.times(E, self.e + 1)


class Unit:

    def __init__(self, kind, blk, pair):
        self.kind, self.blk, self.pair = kind, blk, pair
        self.buf = pair
        self.col = pair * P

    def count(self):
        return self.blk.times(2, self.pair + 1)

    def tile(self):
        return self.blk.times(2, self.pair)


def settle(eng, done, n, sem, value):
    value = value if isinstance(value, int) else eng.snap(value)
    eng.wait_ge(done, n)
    eng.wait_ge(sem, value)


def unit_at(now, slot):
    now = now.back(-(slot // 4))
    slot %= 4
    blk = now if slot < 2 else now.back(LAG)
    return Unit(SELF if slot < 2 else CROSS, blk, slot % 2) if blk.exists() else None


def last_unit(now, slot):
    return next((u for k in range(1, 4) if (u := unit_at(now, slot - k))), None)


def same_buffers(now, slot):
    return next((u for k in (2, 4) if (u := unit_at(now, slot - k))), None)


AHEAD = 6
FIRST, STEADY, LAST = -1, AHEAD + 2, NBLK - 3
END = NBLK + AHEAD + 1


def expert_at(now, slot):
    now = now.back(-(slot // 4))
    off = now.off - AHEAD
    x = Expert(now.i, off // 2, 4 * (off % 2) + slot % 4, now.rounds)
    return x if x.exists() else None


def routed_at(now):
    x = expert_at(now.back(-1), 0)
    return x if x and x.e == 0 else None


def schedule(eng, time):
    for t in range(FIRST, STEADY):
        time(Block(None, t))
    rounds = (LAST + 1 - STEADY) // 2
    with eng.Fori(0, rounds) as i:
        time(Block(i, STEADY, rounds))
        time(Block(i, STEADY + 1, rounds))
    for t in range(STEADY + 2 * rounds, END + 1):
        time(Block(None, t))


def build(nc, x, ctx_in, cst, w, out):
    f32, f16, bf16 = mybir.dt.float32, mybir.dt.float16, mybir.dt.bfloat16
    ALU, ACT, AX = mybir.AluOpType, mybir.ActivationFunctionType, mybir.AxisListType
    st = ExitStack()

    def sb(name, shape, dt=f32):
        return st.enter_context(nc.sbuf_tensor(name, shape, dt))

    def sem(name):
        return st.enter_context(nc.semaphore(name))

    def two(name):
        return [sem(f"{name}_self"), sem(f"{name}_cross")]

    with st:
        consts = sb("consts", [P, C_END])
        ident = consts[:, C_ID:C_ONES]
        head_mask = consts[:, C_HEAD:C_REV]
        rev_idx = consts[:, C_REV:C_END]
        cbf = sb("consts_bf16", [P, C_HEAD], bf16)
        ident_bf, ones_bf = cbf[:, C_ID:C_ONES], cbf[:, C_ONES:C_MKEY]
        mask_key, mask_qry = cbf[:, C_MKEY:C_MQRY], cbf[:, C_MQRY:C_NEG]
        neg_delta, delta = cbf[:, C_NEG:C_DELTA], cbf[:, C_DELTA:C_HEAD]
        wq = [sb(f"wq{a}", [P, D]) for a in range(2)]
        wk = [sb(f"wk{a}", [P, D]) for a in range(2)]
        wv = [sb(f"wv{a}", [P, D]) for a in range(2)]
        wo = [sb(f"wo{a}", [P, D]) for a in range(2)]
        bq = [sb(f"bq{a}", [P, 1]) for a in range(2)]
        bk = [sb(f"bk{a}", [P, 1]) for a in range(2)]
        bv = [sb(f"bv{a}", [P, D]) for a in range(2)]
        bo = [sb(f"bo{a}", [P, D]) for a in range(2)]
        ln_g = [sb(f"ln_g{a}", [P, D]) for a in range(3)]
        ln_b = [sb(f"ln_b{a}", [P, D]) for a in range(3)]
        ln_gc = [sb(f"ln_gc{a}", [P, 1]) for a in range(2)]
        ln_bc = [sb(f"ln_bc{a}", [P, 1]) for a in range(2)]
        b1_bo = sb("b1_bo", [P, D])
        rw = sb("rw", [P, E])
        rb = sb("rb", [P, E])
        w1 = sb("w1", [P, E, FF])
        w2 = sb("w2", [P, E, FC, D])
        b1_rows = sb("b1_rows", [E * FC, P])
        b1 = sb("b1", [P, E * FC])
        b2 = sb("b2", [E, D])

        tok_in = [[sb(f"tok_in{a}{p}", [P, PAIRS, D]) for p in range(2)] for a in range(2)]
        x_bo = [sb(f"x_bo{p}", [P, PAIRS, D]) for p in range(2)]
        inT = [[sb(f"inT{a}{p}", [P, BT]) for p in range(2)] for a in range(2)]
        x1T = [sb(f"x1T{p}", [P, BT]) for p in range(2)]
        x1_bo = sb("x1_bo", [P, TILES, D])
        x2 = sb("x2", [P, TILES, D])
        x2T = sb("x2T", [P, TOK])
        q_hl = [sb(f"q_hl{a}", [P, 2, BT], f16) for a in range(2)]
        k_hl = [sb(f"k_hl{a}", [P, 2, BT], f16) for a in range(2)]
        q_st = [[sb(f"q_st{a}{p}", [P, G, BT], f16) for p in range(2)] for a in range(2)]
        k_st = [sb(f"k_st{a}", [P, G, BT], f16) for a in range(2)]
        k_all = sb("k_all", [P, 4, G * J * BT], f16)
        k_one = [[k_all[:, 2 * a + p, :].rearrange("p (g j t) -> p g j t", g=G, j=J) for p in range(2)] for a in range(2)]
        v_one = [[sb(f"v_one{a}{p}", [P, PAIRS, 2, H, HD + 1]) for p in range(2)] for a in range(2)]
        row_max = [sb(f"row_max{p}", [P, H], bf16) for p in range(2)]
        max_diag = [sb(f"max_diag{p}", [P, HP, S, 2], bf16) for p in range(2)]
        probT = [sb(f"probT{p}", [P, H, S]) for p in range(2)]
        rden = [sb(f"rden{p}", [P, HP, 2]) for p in range(2)]
        o_n = [sb(f"o_n{p}", [P, 2, 2, HP, HD]) for p in range(2)]
        oT = [sb(f"oT{p}", [P, P]) for p in range(2)]
        res = [sb(f"res{p}", [P, D]) for p in range(2)]
        stats = [sb(f"stats{p}", [P, 6]) for p in range(2)]
        mv = [sb(f"mv{p}", [P, 2]) for p in range(2)]
        rstd = [sb(f"rstd{p}", [P, 1]) for p in range(2)]
        veps = [sb(f"veps{p}", [P, 1]) for p in range(2)]
        carrier = sb("carrier", [P, 1])
        eps = sb("eps", [P, MT])
        minus_half = sb("minus_half", [P, MT])
        yn = [sb(f"yn{p}", [P, D]) for p in range(2)]
        yg = [sb(f"yg{p}", [P, D]) for p in range(2)]

        x2_tile = [sb(f"x2_tile{p}", [P, P]) for p in range(2)]
        lg, prob, tmp, oh1, oh2, comb_new = [sb(n, [P, MT, E]) for n in ("lg", "prob", "tmp", "oh1", "oh2", "comb_new")]
        t1, m1, m2, cw1, cw2 = [sb(n, [P, MT]) for n in ("t1", "m1", "m2", "cw1", "cw2")]
        combT = sb("combT", [E, MB])
        comb = sb("comb", [P, MT, E])
        hid = [sb(f"hid{p}", [P, FC, MB]) for p in range(2)]
        acc = sb("acc", [P, MT, D])
        fin = sb("fin", [P, MT, D])
        fst = sb("fst", [P, MT, 6])
        fmv = sb("fmv", [P, MT, 2])
        frs = sb("frs", [P, MT])
        bank = st.enter_context(nc.psum_tensor("bank", [P, 8, 512], f32))
        SC, O_B, TURN, ROW, H_B, Y_B = 0, 2, 3, 4, 5, 7

        q_scr = [[nc.dram_tensor(f"q_scr{a}{p}", [2, P, BT], f16).ap() for p in range(2)] for a in range(2)]
        k_scr = [[nc.dram_tensor(f"k_scr{a}{p}", [2, P, BT], f16).ap() for p in range(2)] for a in range(2)]

        w_in = sem("weights_in")
        moe_in = sem("moe_weights_in")
        cbf_ready = sem("consts_bf16_ready")
        zeroed = sem("v_one_set")
        tok_landed = [[sem(f"tok_landed{a}{p}") for p in range(2)] for a in range(2)]
        xbo_ready = sem("x_bo_ready")
        inT_ready, inT_done = two("inT_ready"), two("inT_done")
        q_ready, k_ready = two("q_ready"), two("k_ready")
        q_hi, k_hi, q_lo, k_lo = two("q_hi"), two("k_hi"), two("q_lo"), two("k_lo")
        q_out, k_out = two("q_out"), two("k_out")
        q_back = [[sem(f"q_back{a}{p}") for p in range(2)] for a in range(2)]
        k_back = two("k_back")
        k_one_ready = two("k_one_ready")
        v_ready, v_done = two("v_ready"), two("v_done")
        s_ready, max_done, diag_ready = two("s_ready"), two("max_done"), two("diag_ready")
        st_ready, exp_done = two("st_ready"), two("exp_done")
        pv_ready, rden_done, on_ready = two("pv_ready"), two("rden_done"), two("on_ready")
        ot_ready, ot_done = two("ot_ready"), two("ot_done")
        wo_ready, res_done = two("wo_ready"), two("res_done")
        ve_done = two("veps_done")
        st_done, mv_done, rs_done, yn_ready = two("stats_done"), two("mv_done"), two("rstd_done"), two("yn_ready")
        yT_ready, yT_done = two("yT_ready"), two("yT_done")
        yg_done, x_done = two("yg_done"), two("x_done")
        x2_tile_ready = sem("x2_tile_ready")
        lg_ready, lg_done, route = sem("lg_ready"), sem("lg_done"), sem("route_step")
        e_ready, e_done, d_ready, d_done = sem("shifted"), sem("shifted_exp"), sem("second_less_first"), sem("its_exp")
        comb_ready, ct_ready, ct_done = sem("comb_ready"), sem("ct_ready"), sem("ct_done")
        b1_ready, b1_done = sem("b1_ready"), sem("b1_done")
        h_ready, h_done = sem("h_ready"), sem("h_done")
        y_ready, y_done = sem("y_ready"), sem("y_done")
        b2_ready, b2_done = sem("b2_ready"), sem("b2_done")
        f_stats, f_mv, f_veps, f_rstd = sem("f_stats"), sem("f_mv"), sem("f_veps"), sem("f_rstd")
        f_norm, f_gain, f_ready, f_out = sem("f_norm"), sem("f_gain"), sem("f_ready"), sem("f_out")

        blk = st.enter_context(nc.Block())
        N_W = [0]

        def tiles_of(v, x):
            n = x.times(MT)
            return v[:, n:n + MT, :] if x.i is None else v[:, bass.ds(n, MT), :]

        def row(v):
            return v.rearrange("(a n) -> a n", a=1)

        @blk.sync
        def _(sp):
            def wait(s, v):
                if not isinstance(v, int):
                    sp.compute_val(v)
                settle(sp, w_in, 16 * N_W[0], s, v)

            def load_tokens(a, b):
                src = (x, ctx_in)[a]
                if not b.exists():
                    return
                if b.back(2).exists():
                    wait(inT_ready[a], b.back(2).times(1, 1))
                    if a == SELF:
                        wait(xbo_ready, b.back(2).times(1, 1))
                n = b.times(BT)
                rows = src[n:n + BT, :] if b.i is None else src[bass.ds(n, BT), :]
                sp.dma_start(tok_in[a][b.par][:, :, :], rows.rearrange("(t p) d -> p t d", p=P)).then_inc(
                    tok_landed[a][b.par], 16)

            def send(a, b, hi, lo, hl, scr, gone):
                wait(hi[a], b.times(1, 1))
                wait(lo[a], b.times(1, 1))
                sp.dma_start(scr[a][b.par].rearrange("s p t -> p s t"), hl[a][:, :, :]).then_inc(gone[a], 16)

            def fetch_q(a, b):
                if b.i is not None:
                    sp.compute_val(b.times(16, 16))
                    sp.compute_val(b.back(2).times(2, 2))
                wait(q_out[a], b.times(16, 16))
                if b.back(2).exists():
                    wait(st_ready[a], b.back(2).times(2, 2))
                for s in range(2):
                    for c in range(2):
                        r = 2 * s + c
                        sp.dma_start(q_st[a][b.par][32 * r:32 * r + 32, :, :],
                                     q_scr[a][b.par][s].rearrange("(g p) t -> p g t", g=G)).then_inc(
                                         q_back[a][b.par], 16)

            def fetch_k(a, b):
                if b.i is not None:
                    sp.compute_val(b.times(16, 16))
                    sp.compute_val(b.back(1).times(1, 1))
                wait(k_out[a], b.times(16, 16))
                if b.back(1).exists():
                    wait(k_one_ready[a], b.back(1).times(1, 1))
                for s in range(2):
                    for c in range(2):
                        r = s + 2 * c
                        sp.dma_start(k_st[a][32 * r:32 * r + 32, :, :],
                                     k_scr[a][b.par][s].rearrange("(g p) t -> p g t", g=G)).then_inc(k_back[a], 16)

            def time(now):
                sa, ca = now.back(-1), now.back(1)
                if now.off >= 0:
                    load_tokens(SELF, now.back(-2))
                    load_tokens(CROSS, now.back(-1))
                if (x := expert_at(now, -5)) and x.e == E - 1:
                    wait(f_ready, x.times(1, 1))
                    n = x.times(MB)
                    rows = out[n:n + MB, :] if x.i is None else out[bass.ds(n, MB), :]
                    sp.dma_start(rows.rearrange("(t p) d -> p t d", p=P), fin[:, :, :]).then_inc(f_out, 16)
                if sa.exists():
                    send(SELF, sa, q_hi, q_lo, q_hl, q_scr, q_out)
                    send(SELF, sa, k_hi, k_lo, k_hl, k_scr, k_out)
                    fetch_q(SELF, sa)
                    fetch_k(SELF, sa)
                if ca.exists():
                    send(CROSS, ca, q_hi, q_lo, q_hl, q_scr, q_out)
                    fetch_q(CROSS, ca)
                    send(CROSS, ca, k_hi, k_lo, k_hl, k_scr, k_out)
                    fetch_k(CROSS, ca)

            def load(dst, src, done=w_in):
                sp.dma_start(dst, src).then_inc(done, 16)
                N_W[0] += done is w_in

            load_tokens(SELF, Block(None, 0))
            load(consts[:, :], cst)
            for a, k in enumerate(("sa", "ca")):
                load(wq[a][:, :], w[f"{k}_wq"])
                load(wk[a][:, :], w[f"{k}_wk"])
                load(wv[a][:, :], w[f"{k}_wv"])
                wop = w[f"{k}_wo"].rearrange("(p h d) n -> h p d n", h=2, d=HD)
                for h in range(2):
                    load(wo[a][64 * h:64 * h + 64, :], wop[h])
                load(bq[a][:, :], w[f"{k}_bq"].rearrange("(p a) -> p a", a=1))
                load(bk[a][:, :], w[f"{k}_bk"].rearrange("(p a) -> p a", a=1))
                load(bv[a][:, :], w[f"{k}_bv"].partition_broadcast(P))
                load(bo[a][:, :], w[f"{k}_bo"].partition_broadcast(P))
                load(ln_gc[a][:, :], w[f"ln{a + 1}_g"].rearrange("(p a) -> p a", a=1))
                load(ln_bc[a][:, :], w[f"ln{a + 1}_b"].rearrange("(p a) -> p a", a=1))
                if a == SELF:
                    load_tokens(SELF, Block(None, 1))
                    load_tokens(CROSS, Block(None, 0))
            for a in range(3):
                load(ln_g[a][:, :], w[f"ln{a + 1}_g"].partition_broadcast(P))
                load(ln_b[a][:, :], w[f"ln{a + 1}_b"].partition_broadcast(P))
            load(rw[:, :], w["router_w"])
            load(rb[:, :], w["router_b"].partition_broadcast(P))
            load(w1[:, :, :], w["e_w1"].rearrange("e d f -> d e f"), moe_in)
            load(w2[:, :, :, :], w["e_w2"].rearrange("e (c f) d -> f e c d", c=FC), moe_in)
            load(b1_rows[:, :], w["e_b1"].rearrange("e (c f) -> (e c) f", c=FC), moe_in)
            load(b2[:, :], w["e_b2"], moe_in)
            schedule(sp, time)

            sp.wait_ge(f_out, 16 * ROUNDS)

        @blk.gpsimd
        def _(pool):
            for a in range(2):
                for p in range(2):
                    pool.memset(v_one[a][p][:, :, :, :, :], 0.0).then_inc(zeroed, 1)
            for p in range(2):
                pool.memset(o_n[p][:, :, :, :, :], 0.0).then_inc(zeroed, 1)
            pool.memset(minus_half[:, :], -0.5).then_inc(zeroed, 1)
            pool.memset(eps[:, :], EPS).then_inc(zeroed, 1)
            pool.wait_ge(zeroed, 8)
            for a in range(2):
                for p in range(2):
                    for b in range(2):
                        pool.memset(v_one[a][p][64 * b:64 * b + 64, :, b, :, HD:HD + 1], 1.0).then_inc(zeroed, 1)
                        pool.wait_ge(zeroed, 8 + 4 * a + 2 * p + b + 1)
            pool.wait_ge(zeroed, 16)
            pool.wait_ge(w_in, 16 * N_W[0])
            pool.tensor_tensor(b1_bo[:, :], ln_b[0][:, :], bo[CROSS][:, :], ALU.add).then_inc(zeroed, 1)
            pool.wait_ge(zeroed, 17)

            def add_bo(b):
                pool.wait_ge(tok_landed[SELF][b.par], b.landed())
                if b.back(2).exists():
                    pool.wait_ge(res_done[SELF], b.back(2).times(2, 2))
                pool.tensor_tensor(x_bo[b.par][:, :, :], tok_in[SELF][b.par][:, :, :],
                                   bo[SELF][:, :].unsqueeze(1).to_broadcast([P, PAIRS, D]), ALU.add).then_inc(xbo_ready, 1)

            def spread(u):
                a, n = u.kind, u.buf
                pool.wait_ge(mv_done[a], u.count())
                pool.tensor_tensor(veps[n][:, :], mv[n][:, 1:2], eps[:, 0:1], ALU.add).then_inc(ve_done[a], 1)
                pool.wait_ge(ve_done[a], u.count())
                pool.tensor_tensor(rstd[n][:, :], veps[n][:, :], minus_half[:, 0:1], ALU.pow).then_inc(rs_done[a], 1)

            def gain(u):
                a = u.kind
                pool.wait_ge(yn_ready[a], u.count())
                pool.tensor_tensor(yg[u.buf][:, :], yn[u.buf][:, :], ln_g[a][:, :], ALU.mult).then_inc(yg_done[a], 1)
                pool.wait_ge(yg_done[a], u.count())
                dst = (x1_bo, x2)[a][:, u.tile(), :]
                off = (b1_bo, ln_b[1])[a]
                pool.tensor_tensor(dst, yg[u.buf][:, :], off[:, :], ALU.add).then_inc(x_done[a], 1)

            def last_spread(x):
                pool.wait_ge(f_mv, x.times(1, 1))
                pool.tensor_tensor(frs[:, :], fmv[:, :, 1], eps[:, :], ALU.add).then_inc(f_veps, 1)
                pool.wait_ge(f_veps, x.times(1, 1))
                pool.tensor_tensor(frs[:, :], frs[:, :], minus_half[:, :], ALU.pow).then_inc(f_rstd, 1)

            def last_gain(x):
                pool.wait_ge(f_norm, x.times(1, 1))
                pool.tensor_tensor(fin[:, :, :], fin[:, :, :], ln_g[2][:, :].unsqueeze(1).to_broadcast([P, MT, D]),
                                   ALU.mult).then_inc(f_gain, 1)
                pool.wait_ge(f_gain, x.times(1, 1))
                pool.tensor_tensor(fin[:, :, :], fin[:, :, :], ln_b[2][:, :].unsqueeze(1).to_broadcast([P, MT, D]),
                                   ALU.add).then_inc(f_ready, 1)

            def time(now):
                for s in range(4):
                    if s == 0 and now.back(-1).exists():
                        add_bo(now.back(-1))
                    if u := unit_at(now, s - 4):
                        gain(u)
                    if u := unit_at(now, s - 3):
                        spread(u)
                    if (x := expert_at(now, s - 1)) and x.e == E - 1:
                        last_spread(x)
                    if (x := expert_at(now, s - 2)) and x.e == E - 1:
                        last_gain(x)

            schedule(pool, time)

        @blk.scalar
        def _(act):
            act.wait_ge(w_in, 16 * N_W[0])

            def turned(a, b):
                act.wait_ge(inT_ready[a], b.times(1, 1))
                if b.back(2).exists():
                    act.wait_ge(v_ready[a], b.back(2).times(1, 1))
                act.activation(inT[a][b.par][:, :], bank[:, TURN, a * BT:(a + 1) * BT], ACT.Copy).then_inc(inT_done[a], 1)

            def high(a, b, ready, hi, hl, bias, gone, half=0):
                act.wait_ge(ready[a], b.times(1, 1))
                if b.back(1).exists():
                    act.wait_ge(gone[a], b.times(16))
                act.activation(hl[a][:, 0, :], bank[:, ROW, half * BT:(half + 1) * BT], ACT.Identity, bias=bias[a][:, :]).then_inc(hi[a], 1)

            def exps(u, v):
                a = u.kind
                act.wait_ge(st_ready[a], u.count())
                if v:
                    act.wait_ge(pv_ready[v.kind], v.count())
                act.activation(probT[u.buf][:, :, :].rearrange("p h q -> p (h q)"),
                               bank[:, SC:SC + 2, :].rearrange("p a n -> p (a n)"), ACT.Exp,
                               scale=float(HD) ** -0.5).then_inc(exp_done[a], 1)

            def o_turned(u, v):
                a = u.kind
                act.wait_ge(ot_ready[a], u.count())
                if v:
                    act.wait_ge(wo_ready[v.kind], v.count())
                act.activation(oT[u.buf][:, :], bank[:, TURN, 0:P], ACT.Copy).then_inc(ot_done[a], 1)

            def y_turned(u):
                a, b = u.kind, u.blk
                act.wait_ge(yT_ready[a], u.count())
                if a == SELF:
                    if b.back(2).exists():
                        act.wait_ge(q_ready[CROSS], b.back(2).times(1, 1))
                    act.activation(x1T[b.par][:, u.col:u.col + P], bank[:, TURN, 0:P], ACT.Identity,
                                   bias=ln_bc[a][:, :], scale=ln_gc[a][:, :]).then_inc(yT_done[a], 1)
                    return
                if b.back(1).exists():
                    act.wait_ge(lg_ready, Unit(CROSS, b.back(1), u.pair).count())
                act.activation(x2_tile[u.buf][:, :], bank[:, TURN, 0:P], ACT.Identity,
                               bias=ln_bc[a][:, :], scale=ln_gc[a][:, :]).then_inc(x2_tile_ready, 1)
                n = b.times(BT, u.col)
                act.activation(x2T[:, n:n + P] if b.i is None else x2T[:, bass.ds(n, P)], bank[:, TURN, 0:P],
                               ACT.Identity, bias=ln_bc[a][:, :], scale=ln_gc[a][:, :]).then_inc(yT_done[a], 1)

            def gelus(x, chunks):
                for c in chunks:
                    k = x.e * FC + c
                    act.wait_ge(h_ready, x.times(E * FC, k + 1))
                    if c == 0 and not x.early(2):
                        act.wait_ge(y_ready, x.times(E, x.e - 1))
                    act.activation(hid[x.e % 2][:, c, :], bank[:, H_B + c % 2, :], ACT.Gelu,
                                   bias=b1[:, k:k + 1]).then_inc(h_done, 1)

            def time(now):
                sa, ca = now.back(-1), now.back(1)
                r = routed_at(now)
                for s in range(4):
                    x = expert_at(now, s)
                    if s == 0 and now.i is None and now.off == AHEAD - 1:
                        act.wait_ge(b1_ready, 1)
                        act.activation(b1[:, :], bank[:, Y_B, 0:E * FC], ACT.Copy).then_inc(b1_done, 1)
                        act.wait_ge(b1_done, 1)
                    if u := unit_at(now, s - 3):
                        o_turned(u, same_buffers(now, s - 3))
                    if x:
                        gelus(x, (0, 1, 2, 3))
                    if u := unit_at(now, s - 4):
                        y_turned(u)
                    if u := unit_at(now, s - 1):
                        exps(u, same_buffers(now, s - 1))
                    if s == 0:
                        if ca.exists():
                            act.wait_ge(inT_ready[CROSS], ca.times(1, 1))
                        if sa.exists():
                            turned(SELF, sa)
                        if ca.exists():
                            turned(CROSS, ca)
                    if s == 1 and sa.exists():
                        act.wait_ge(k_ready[SELF], sa.times(1, 1))
                        high(SELF, sa, q_ready, q_hi, q_hl, bq, q_out)
                        high(SELF, sa, k_ready, k_hi, k_hl, bk, k_out, 1)
                    if s == 2 and ca.exists():
                        if sa.exists():
                            act.wait_ge(v_ready[SELF], sa.times(1, 1))
                        high(CROSS, ca, q_ready, q_hi, q_hl, bq, q_out)
                    if s == 3 and ca.exists():
                        act.wait_ge(v_ready[CROSS], ca.times(1, 1))
                        high(CROSS, ca, k_ready, k_hi, k_hl, bk, k_out)
                    if r and s == 1:
                        act.wait_ge(e_ready, r.times(1, 1))
                        act.activation(tmp[:, :, :], lg[:, :, :], ACT.Exp).then_inc(e_done, 1)
                    if r and s == 2:
                        act.wait_ge(d_ready, r.times(1, 1))
                        act.activation(t1[:, :], m2[:, :], ACT.Exp).then_inc(d_done, 1)
                    if r and s == 3:
                        act.wait_ge(ct_ready, r.times(1, 1))
                        act.activation(combT[:, :], bank[0:E, TURN, :], ACT.Copy).then_inc(ct_done, 1)

            schedule(act, time)

        @blk.vector
        def _(dve):
            dve.wait_ge(w_in, 16 * N_W[0])
            dve.tensor_copy(cbf[:, :], consts[:, 0:C_HEAD]).then_inc(cbf_ready, 1)
            dve.wait_ge(cbf_ready, 1)
            dve.wait_ge(zeroed, 17)

            def low(a, b, hi, lo, hl, bias, half=0):
                dve.wait_ge(hi[a], b.times(1, 1))
                dve.scalar_tensor_tensor(hl[a][:, 1, :], bank[:, ROW, half * BT:(half + 1) * BT], bias[a][:, :], hl[a][:, 0, :],
                                         ALU.add, ALU.subtract).then_inc(lo[a], 1)

            def masks(a, b):
                dve.wait_ge(k_back[a], b.times(64, 64))
                if b.back(2).exists():
                    dve.wait_ge(st_ready[a], b.back(2).times(2, 2))
                for j in range(J):
                    last = dve.tensor_scalar(k_one[a][b.par][:, :, j, :], k_st[a][:, :, :],
                                             head_mask[:, j:j + 1], None, ALU.mult)
                last.then_inc(k_one_ready[a], 1)

            def v_rows(a, b):
                dve.wait_ge(v_ready[a], b.times(1, 1))
                if b.back(2).exists():
                    dve.wait_ge(pv_ready[a], b.back(2).times(2, 2))
                for h in range(2):
                    r = slice(64 * h, 64 * h + 64)
                    last = dve.tensor_tensor(
                        v_one[a][b.par][r, :, h, :, 0:HD],
                        bank[r, ROW, BT:2 * BT].rearrange("p (t h d) -> p t h d", t=PAIRS, h=H),
                        bv[a][r, :].rearrange("p (h d) -> p h d", h=H).unsqueeze(1).to_broadcast([64, PAIRS, H, HD]),
                        ALU.add)
                last.then_inc(v_done[a], 1)

            def maxima(u):
                a = u.kind
                dve.wait_ge(s_ready[a], u.count())
                dve.reduce_max(row_max[u.buf][:, :],
                               bank[:, SC:SC + 2, :].rearrange("p a (h k) -> p (a h) k", k=S), AX.X).then_inc(max_done[a], 1)
                dve.wait_ge(max_done[a], u.count())
                m = row_max[u.buf][:, :].rearrange("p (a c) -> p a c", c=2).unsqueeze(2).to_broadcast([P, HP, S, 2])
                dl = neg_delta.rearrange("p (q c) -> p q c", c=2).unsqueeze(1).to_broadcast([P, HP, S, 2])
                dve.tensor_tensor(max_diag[u.buf][:, :, :, :], dl, m, ALU.mult).then_inc(diag_ready[a], 1)

            def outputs(u):
                a = u.kind
                dve.wait_ge(pv_ready[a], u.count())
                o = bank[:, O_B, 0:HP * 36].rearrange("p (a b c d) -> p a b c d", a=HP, b=2, c=2)
                for h in range(2):
                    r = slice(64 * h, 64 * h + 64)
                    last = dve.reciprocal(rden[u.buf][r, :, :], o[r, :, :, h, HD])
                last.then_inc(rden_done[a], 1)
                dve.wait_ge(rden_done[a], u.count())
                for h in range(2):
                    r = slice(64 * h, 64 * h + 64)
                    last = dve.tensor_tensor(o_n[u.buf][r, :, h, :, :].rearrange("p b a d -> p a b d"), o[r, :, :, h, 0:HD],
                                             rden[u.buf][r, :, :].unsqueeze(3).to_broadcast([64, HP, 2, HD]), ALU.mult)
                last.then_inc(on_ready[a], 1)

            def residual(u):
                a, n = u.kind, u.buf
                dve.wait_ge(wo_ready[a], u.count())
                if a == SELF:
                    dve.wait_ge(xbo_ready, u.blk.times(1, 1))
                    r = x_bo[u.blk.par][:, u.pair, :]
                else:
                    dve.wait_ge(x_done[SELF], u.count())
                    r = x1_bo[:, u.tile(), :]
                dve.tensor_tensor(res[n][:, :], bank[:, ROW, 0:D], r, ALU.add).then_inc(res_done[a], 1)
                dve.wait_ge(res_done[a], u.count())
                dve.bn_stats(stats[n][:, :], res[n][:, :]).then_inc(st_done[a], 1)
                dve.wait_ge(st_done[a], u.count())
                dve.tensor_copy(carrier[:, :], consts[:, 0:1])
                dve.bn_aggr(mv[n][:, :], stats[n][:, :]).then_inc(mv_done[a], 1)

            def norm(u, v):
                a, n = u.kind, u.buf
                dve.wait_ge(rs_done[a], u.count())
                if v:
                    dve.wait_ge(yT_ready[v.kind], v.count())
                    dve.wait_ge(yg_done[v.kind], v.count())
                dve.tensor_scalar(yn[n][:, :], res[n][:, :], mv[n][:, 0:1], rstd[n][:, :], ALU.subtract,
                                  ALU.mult).then_inc(yn_ready[a], 1)

            def wide(v):
                return v[:, :].unsqueeze(2).to_broadcast([P, MT, E])

            class Steps:

                def __init__(self, x, done):
                    self.x, self.done = x, done

                def __call__(self, ins):
                    self.done += 1
                    ins.then_inc(route, 1)
                    dve.wait_ge(route, self.x.times(ROUTE_STEPS, self.done))

            def logits(u):
                dve.wait_ge(lg_ready, u.count())
                dve.tensor_tensor(lg[:, 2 * u.blk.par + u.pair, :], bank[:, ROW, 0:E], rb[:, :], ALU.add).then_inc(lg_done, 1)

            def route_logits(x):
                step = Steps(x, 0)
                dve.wait_ge(lg_done, x.times(MT, MT))
                step(dve.reduce_max(t1[:, :], lg[:, :, :], AX.X))
                dve.tensor_tensor(lg[:, :, :], lg[:, :, :], wide(t1), ALU.subtract).then_inc(e_ready, 1)

            def first_of(step, m):
                step(dve.reduce_max(m[:, :], prob[:, :, :], AX.X))
                step(dve.tensor_tensor(tmp[:, :, :], prob[:, :, :], wide(m), ALU.is_equal))
                step(dve.tensor_tensor(tmp[:, :, :], tmp[:, :, :],
                                       rev_idx.unsqueeze(1).to_broadcast([P, MT, E]), ALU.mult))
                step(dve.reduce_max(t1[:, :], tmp[:, :, :], AX.X))

            def route_probs(x):
                step = Steps(x, 1)
                dve.wait_ge(e_done, x.times(1, 1))
                step(dve.reduce_sum(t1[:, :], tmp[:, :, :], AX.X))
                step(dve.reciprocal(t1[:, :], t1[:, :]))
                step(dve.tensor_tensor(prob[:, :, :], tmp[:, :, :], wide(t1), ALU.mult))
                first_of(step, m1)
                step(dve.tensor_tensor(oh1[:, :, :], tmp[:, :, :], wide(t1), ALU.is_equal))
                step(dve.scalar_tensor_tensor(prob[:, :, :].rearrange("p t e -> p (t e)"),
                                              oh1[:, :, :].rearrange("p t e -> p (t e)"), -2.0,
                                              prob[:, :, :].rearrange("p t e -> p (t e)"), ALU.mult, ALU.add))
                first_of(step, m2)
                step(dve.tensor_tensor(oh2[:, :, :], tmp[:, :, :], wide(t1), ALU.is_equal))
                dve.tensor_tensor(m2[:, :], m2[:, :], m1[:, :], ALU.subtract).then_inc(d_ready, 1)

            def route_weights(x):
                step = Steps(x, 15)
                dve.wait_ge(d_done, x.times(1, 1))
                step(dve.tensor_scalar(cw1[:, :], t1[:, :], 1.0, None, ALU.add))
                step(dve.reciprocal(cw1[:, :], cw1[:, :]))
                step(dve.tensor_tensor(cw2[:, :], t1[:, :], cw1[:, :], ALU.mult))
                step(dve.tensor_tensor(oh1[:, :, :], oh1[:, :, :], wide(cw1), ALU.mult))
                step(dve.tensor_tensor(oh2[:, :, :], oh2[:, :, :], wide(cw2), ALU.mult))
                step(dve.tensor_tensor(comb_new[:, :, :], oh1[:, :, :], oh2[:, :, :], ALU.add))

            def add_b2(x):
                dve.wait_ge(x_done[CROSS], x.times(MT, MT))
                dve.wait_ge(b2_ready, x.times(1, 1))
                dve.tensor_tensor(tiles_of(x2, x), tiles_of(x2, x), bank[:, Y_B, :].rearrange("p (t d) -> p t d", t=MT),
                                  ALU.add).then_inc(b2_done, 1)

            def combine(x):
                if x.e == 0:
                    dve.tensor_copy(comb[:, :, :], comb_new[:, :, :]).then_inc(comb_ready, 1)
                    dve.wait_ge(b2_done, x.times(1, 1))
                    dve.wait_ge(comb_ready, x.times(1, 1))
                    if not x.early(1):
                        dve.wait_ge(f_norm, x.times(1))
                else:
                    dve.wait_ge(y_done, x.times(E, x.e))
                dve.wait_ge(y_ready, x.count())
                n = x.times(MT)
                for t in range(MT):
                    last = dve.scalar_tensor_tensor(acc[:, t, :], bank[:, Y_B, t * D:(t + 1) * D], comb[:, t, x.e:x.e + 1],
                                                    acc[:, t, :] if x.e else x2[:, n + t, :], ALU.mult, ALU.add)
                last.then_inc(y_done, 1)

            def last_stats(x):
                dve.wait_ge(y_done, x.count())
                for t in range(MT):
                    last = dve.bn_stats(fst[:, t, :], acc[:, t, :])
                last.then_inc(f_stats, 1)
                dve.wait_ge(f_stats, x.times(1, 1))
                dve.tensor_copy(carrier[:, :], consts[:, 0:1])
                for t in range(MT):
                    last = dve.bn_aggr(fmv[:, t, :], fst[:, t, :])
                last.then_inc(f_mv, 1)

            def last_norm(x):
                dve.wait_ge(f_rstd, x.times(1, 1))
                if not x.early(E):
                    dve.wait_ge(f_out, x.times(16))
                for t in range(MT):
                    last = dve.tensor_scalar(fin[:, t, :], acc[:, t, :], fmv[:, t, 0:1], frs[:, t:t + 1], ALU.subtract,
                                             ALU.mult)
                last.then_inc(f_norm, 1)

            def time(now):
                sa, ca = now.back(-1), now.back(1)
                r = routed_at(now)
                for s in range(4):
                    x, y = expert_at(now, s - 1), expert_at(now, s - 2)
                    if u := unit_at(now, s):
                        maxima(u)
                    if u := unit_at(now, s - 2):
                        outputs(u)
                    if u := unit_at(now, s - 3):
                        residual(u)
                    if s == 0 and (q := expert_at(now, 0)) and q.e == 0:
                        add_b2(q)
                    if y and y.e == E - 1:
                        last_norm(y)
                    if r and s == 2:
                        route_weights(r)
                    if u := unit_at(now, s - 3):
                        norm(u, same_buffers(now, s - 3))
                    if s == 1 and sa.exists():
                        dve.wait_ge(k_hi[SELF], sa.times(1, 1))
                        low(SELF, sa, q_hi, q_lo, q_hl, bq)
                        low(SELF, sa, k_hi, k_lo, k_hl, bk, 1)
                    if s == 2 and ca.exists():
                        low(CROSS, ca, q_hi, q_lo, q_hl, bq)
                    if s == 3 and ca.exists():
                        low(CROSS, ca, k_hi, k_lo, k_hl, bk)
                    if s == 2 and sa.exists():
                        v_rows(SELF, sa)
                    if s == 3 and ca.exists():
                        v_rows(CROSS, ca)
                    if s == 3 and sa.exists():
                        masks(SELF, sa)
                    if s == 1 and ca.back(1).exists():
                        masks(CROSS, ca.back(1))
                    if x:
                        combine(x)
                        if x.e == E - 1:
                            last_stats(x)
                    if (u := unit_at(now, s - 5)) and u.kind == CROSS:
                        logits(u)
                    if r and s == 0:
                        route_logits(r)
                    if r and s == 1:
                        route_probs(r)

            schedule(dve, time)

        @blk.tensor
        def _(pe):
            pe.wait_ge(cbf_ready, 1)

            def after(now, s, part, parts, reader):
                order = [(q, k) for q in range(s - 8, s + 1) for k in parts]
                for q, k in reversed(order[:order.index((s, part))]):
                    if found := reader(now.back(-(q // 4)), q, q % 4, k):
                        pe.wait_ge(*found)
                        return

            def turn_free(now, s, part):
                def reader(t, q, r, k):
                    if k == "o" and (u := unit_at(now, q - 3)):
                        return ot_done[u.kind], u.count()
                    if k == "y" and (u := unit_at(now, q - 4)):
                        return yT_done[u.kind], u.count()
                    if k == "inputs" and r == 0 and t.back(1).exists():
                        return inT_done[CROSS], t.back(1).times(1, 1)
                    if k == "inputs" and r == 0 and t.back(-1).exists():
                        return inT_done[SELF], t.back(-1).times(1, 1)
                    if k == "comb" and r == 3 and (x := routed_at(t)):
                        return ct_done, x.times(1, 1)
                after(now, s, part, ("o", "y", "inputs", "comb"), reader)

            def row_free(now, s, part):
                def reader(t, q, r, k):
                    sa, ca = t.back(-1), t.back(1)
                    if k == "wo" and (u := unit_at(now, q - 3)):
                        return res_done[u.kind], u.count()
                    if k == "prepared" and r == 1 and sa.exists():
                        return k_lo[SELF], sa.times(1, 1)
                    if k == "prepared" and r == 2 and sa.exists():
                        return v_done[SELF], sa.times(1, 1)
                    if k == "prepared" and r == 2 and ca.exists():
                        return q_lo[CROSS], ca.times(1, 1)
                    if k == "prepared" and r == 3 and ca.exists():
                        return v_done[CROSS], ca.times(1, 1)
                    if k == "logits" and (u := unit_at(now, q - 5)) and u.kind == CROSS:
                        return lg_done, u.count()
                after(now, s, part, ("wo", "prepared", "logits"), reader)

            def scores_free(now, s, part):
                def reader(t, q, r, k):
                    if k == "queries" and (u := unit_at(now, q)):
                        return max_done[u.kind], u.count()
                    if k == "keys" and (u := unit_at(now, q - 1)):
                        return exp_done[u.kind], u.count()
                after(now, s, part, ("queries", "keys"), reader)

            def sums_free(now, s, part):
                def reader(t, q, r, k):
                    if k == "down" and (x := expert_at(now, q - 1)):
                        return y_done, x.count()
                    if k == "b2" and r == 3 and (x := routed_at(t)):
                        return b2_done, x.times(1, 1)
                after(now, s, part, ("down", "b2"), reader)

            def turn_in(a, b):
                pe.wait_ge(tok_landed[a][b.par], b.landed())
                for t in range(PAIRS):
                    last = pe.transpose(bank[:, TURN, a * BT + t * P:a * BT + (t + 1) * P], tok_in[a][b.par][:, t, :], ident)
                last.then_inc(inT_ready[a], 1)

            def project(wt, src, ready, a, half=0):
                pe.matmul(bank[:, ROW, half * BT:(half + 1) * BT], wt[a][:, :], src[:, :], start=True, stop=True).then_inc(ready[a], 1)

            def v_proj(a, b):
                for t in range(PAIRS):
                    last = pe.matmul(bank[:, ROW, BT + t * P:BT + (t + 1) * P], inT[a][b.par][:, t * P:(t + 1) * P], wv[a][:, :],
                                     start=True, stop=True)
                last.then_inc(v_ready[a], 1)

            def scores(now, s, u):
                a, b = u.kind, u.blk
                pe.wait_ge(q_back[a][b.par], b.landed(64))
                pe.wait_ge(k_one_ready[a], b.times(1, 1))
                scores_free(now, s, "queries")
                q, k = q_st[a][b.par], k_one[a][b.par]
                for n in range(2):
                    if a == SELF:
                        pe.matmul(bank[:, SC + n, :], ident_bf, mask_key.unsqueeze(1).to_broadcast([P, H // 2, S]),
                                  start=True, stop=True)
                    for gi in range(2):
                        for h in range(2):
                            c = u.col + 64 * h
                            last = pe.matmul(bank[64 * h:64 * h + 64, SC + n, 256 * gi:256 * gi + 256],
                                             q[:, 2 * n + gi, c:c + 64], k[:, 2 * n + gi, :, c:c + 64],
                                             start=a == CROSS and gi == 0, stop=True, skip_group_check=True)
                last.then_inc(s_ready[a], 1)

            def scores_T(now, s, u):
                a, b = u.kind, u.blk
                pe.wait_ge(diag_ready[a], u.count())
                scores_free(now, s, "keys")
                q, k = q_st[a][b.par], k_one[a][b.par]
                for n in range(2):
                    pe.matmul(bank[:, SC + n, :], ones_bf,
                              max_diag[u.buf][:, 4 * n:4 * n + 4, :, :].rearrange("p a q c -> p a c q"),
                              start=True, stop=True)
                    if a == SELF:
                        pe.matmul(bank[:, SC + n, :], mask_qry, delta.unsqueeze(1).to_broadcast([P, H // 2, S]),
                                  start=False, stop=True, skip_group_check=True)
                    for hh in range(H // 2):
                        g, j = divmod(8 * n + hh, J)
                        for h in range(2):
                            c = u.col + 64 * h
                            last = pe.matmul(bank[64 * h:64 * h + 64, SC + n, 64 * hh:64 * hh + 64],
                                             k[:, g, j, c:c + 64], q[:, g, c:c + 64],
                                             start=False, stop=True, skip_group_check=True)
                last.then_inc(st_ready[a], 1)

            def weigh(u, v):
                a, b = u.kind, u.blk
                pe.wait_ge(exp_done[a], u.count())
                pe.wait_ge(v_done[a], b.times(1, 1))
                if v:
                    pe.wait_ge(on_ready[v.kind], v.count())
                for p in range(HP):
                    last = pe.matmul(bank[:, O_B, 36 * p:36 * p + 36],
                                     probT[u.buf][:, 2 * p:2 * p + 2, :].rearrange("p h q -> p (h q)"),
                                     v_one[a][b.par][:, u.pair, :, 2 * p:2 * p + 2, :].rearrange("p b h d -> p b (h d)"),
                                     start=True, stop=True)
                last.then_inc(pv_ready[a], 1)

            def turn_o(now, s, u):
                turn_free(now, s, "o")
                pe.wait_ge(on_ready[u.kind], u.count())
                for b in range(2):
                    last = pe.matmul(bank[:, TURN, 64 * b:64 * b + 64],
                                     o_n[u.buf][:, b, :, :, :].rearrange("p c a d -> p (c a d)"),
                                     consts[:, C_DELTA:C_HEAD], start=True, stop=True)
                last.then_inc(ot_ready[u.kind], 1)

            def out_proj(now, s, u):
                pe.wait_ge(ot_done[u.kind], u.count())
                row_free(now, s, "wo")
                pe.matmul(bank[:, ROW, 0:D], oT[u.buf][:, :], wo[u.kind][:, :], start=True, stop=True).then_inc(
                    wo_ready[u.kind], 1)

            def turn_y(now, s, u):
                pe.wait_ge(yn_ready[u.kind], u.count())
                turn_free(now, s, "y")
                pe.transpose(bank[:, TURN, 0:P], yn[u.buf][:, :], ident).then_inc(yT_ready[u.kind], 1)

            def logits(now, s, u):
                pe.wait_ge(x2_tile_ready, u.count())
                row_free(now, s, "logits")
                pe.matmul(bank[:, ROW, 0:E], x2_tile[u.buf][:, :], rw[:, :], start=True, stop=True).then_inc(lg_ready, 1)

            def out_bias(now, s, x):
                turn_free(now, s, "comb")
                pe.wait_ge(route, x.times(ROUTE_STEPS, ROUTE_STEPS))
                for t in range(MT):
                    last = pe.transpose(bank[0:E, TURN, t * P:(t + 1) * P], comb_new[:, t, :], ident)
                last.then_inc(ct_ready, 1)
                sums_free(now, s, "b2")
                pe.wait_ge(ct_done, x.times(1, 1))
                for t in range(MT):
                    last = pe.matmul(bank[:, Y_B, t * D:(t + 1) * D], combT[:, t * P:(t + 1) * P], b2[:, :],
                                     start=True, stop=True)
                last.then_inc(b2_ready, 1)

            def up(x, chunks):
                if x.e == 0 and chunks[0] == 0:
                    pe.wait_ge(yT_done[CROSS], x.times(MT, MT))
                n = x.times(MB)
                src = x2T[:, n:n + MB] if x.i is None else x2T[:, bass.ds(n, MB)]
                for c in chunks:
                    if not (x.early(1) and c < 2):
                        pe.wait_ge(h_done, x.times(E * FC, x.e * FC + c - 1))
                    pe.matmul(bank[:, H_B + c % 2, :], w1[:, x.e, c * P:(c + 1) * P], src, start=True, stop=True).then_inc(
                        h_ready, 1)

            def down(now, s, x, tiles):
                if tiles[0] == 0:
                    pe.wait_ge(h_done, x.times(E * FC, x.e * FC + FC))
                    sums_free(now, s, "down")
                for t in tiles:
                    for c in range(FC):
                        last = pe.matmul(bank[:, Y_B, t * D:(t + 1) * D], hid[x.e % 2][:, c, t * P:(t + 1) * P],
                                         w2[:, x.e, c, :], start=c == 0, stop=c == FC - 1, skip_group_check=True)
                if tiles[-1] == MT - 1:
                    last.then_inc(y_ready, 1)

            def time(now):
                sa, ca = now.back(-1), now.back(1)
                for s in range(4):
                    x, y = expert_at(now, s), expert_at(now, s - 1)
                    if s == 0 and now.i is None and now.off == AHEAD - 1:
                        pe.wait_ge(moe_in, 64)
                        pe.transpose(bank[:, Y_B, 0:E * FC], b1_rows[:, :], ident[0:E * FC, 0:E * FC]).then_inc(b1_ready, 1)
                        pe.wait_ge(b1_done, 1)
                    if u := unit_at(now, s - 3):
                        turn_o(now, s, u)
                    if x:
                        up(x, (0, 1))
                    if u := unit_at(now, s):
                        scores(now, s, u)
                    if u := unit_at(now, s - 2):
                        weigh(u, last_unit(now, s - 2))
                    if u := unit_at(now, s - 3):
                        out_proj(now, s, u)
                    if x:
                        up(x, (2, 3))
                    if u := unit_at(now, s - 4):
                        turn_y(now, s, u)
                    if u := unit_at(now, s - 1):
                        scores_T(now, s, u)
                    if s == 0 and (sa.exists() or ca.exists()):
                        turn_free(now, s, "inputs")
                        if sa.exists():
                            turn_in(SELF, sa)
                        if ca.exists():
                            turn_in(CROSS, ca)
                    if s == 1 and sa.exists():
                        row_free(now, s, "prepared")
                        pe.wait_ge(inT_done[SELF], sa.times(1, 1))
                        project(wq, inT[SELF][sa.par], q_ready, SELF)
                        project(wk, inT[SELF][sa.par], k_ready, SELF, 1)
                    if s == 2 and (sa.exists() or ca.exists()):
                        row_free(now, s, "prepared")
                        if ca.exists():
                            pe.wait_ge(yT_done[SELF], ca.times(2, 2))
                            project(wq, x1T[ca.par], q_ready, CROSS)
                        if sa.exists():
                            v_proj(SELF, sa)
                    if s == 3 and ca.exists():
                        row_free(now, s, "prepared")
                        pe.wait_ge(inT_done[CROSS], ca.times(1, 1))
                        project(wk, inT[CROSS][ca.par], k_ready, CROSS)
                        v_proj(CROSS, ca)
                    if y:
                        down(now, s, y, (0, 1))
                    if y:
                        down(now, s, y, (2, 3))
                    if (u := unit_at(now, s - 5)) and u.kind == CROSS:
                        logits(now, s, u)
                    if s == 3 and (r := routed_at(now)):
                        out_bias(now, s, r)

            schedule(pe, time)


_INS = ['x', 'ctx_1024', 'sa_wq', 'sa_bq', 'sa_wk', 'sa_bk', 'sa_wv', 'sa_bv', 'sa_wo', 'sa_bo', 'ca_wq', 'ca_bq', 'ca_wk',
        'ca_bk', 'ca_wv', 'ca_bv', 'ca_wo', 'ca_bo', 'ln1_g', 'ln1_b', 'ln2_g', 'ln2_b', 'ln3_g', 'ln3_b', 'router_w',
        'router_b', 'e_w1', 'e_b1', 'e_w2', 'e_b2']


def kernel(**inputs):
    import numpy as _np
    import concourse.bacc as _bacc
    from concourse import mybir as _mybir
    from concourse.bass_utils import run_bass_kernel_spmd as _run

    nc = _bacc.Bacc("TRN2", target_bir_lowering=False, num_devices=1)
    arrays, aps = {}, {}

    def give(name, a):
        arrays[f"in_{name}"] = _np.ascontiguousarray(a)
        aps[name] = nc.dram_tensor(f"in_{name}", a.shape, _mybir.dt.from_np(a.dtype), kind="ExternalInput").ap()

    for name in _INS:
        a = _np.asarray(inputs[name if name in ("x", "ctx_1024") else "L0_xattn_" + name])
        give(name, a.reshape(TOK, D) if name in ("x", "ctx_1024") else a)
    give("consts", shape_constants())
    out = nc.dram_tensor("out", (TOK, D), _mybir.dt.float32, kind="ExternalOutput").ap()
    build(nc, aps["x"], aps["ctx_1024"], aps["consts"], aps, out)
    r = _run(nc, [arrays], core_ids=[0])
    return r.results[0]["out"].reshape(B, S, D)
```

```python
import numpy as np
import concourse.bass as bass
from concourse import mybir
from contextlib import ExitStack

B, S, D, H, FF, E = 64, 64, 128, 16, 512, 8
HD = D // H
P = 128
TOK = B * S
TILES = TOK // P
PAIRS = 2
BT = PAIRS * P
NBLK = TOK // BT
G = 4
J = H // G
HP = H // 2
SELF, CROSS = 0, 1
LAG = 2
EPS = 1e-5
MASKED = -1e30
FC = FF // P
MB = 512
MT = MB // P
ROUNDS = TOK // MB
W1_SCALE = 64.0
W1_TIMES = (2, 3)
DVE_HEADS = 10
ROUTE_STEPS = 21

C_ID, C_ONES, C_MKEY, C_MQRY, C_NEG, C_DELTA, C_HEAD, C_REV, C_END = np.cumsum(
    [0, P, P, S, P, 2 * S, S, J, E]).tolist()


def shape_constants():
    c = np.zeros((P, C_END), np.float32)
    p = np.arange(P)
    batch, tok = p // S, p % S
    same = batch[:, None] == batch[None, :]
    c[:, C_ID:C_ONES] = np.eye(P)
    c[:, C_ONES:C_MKEY] = same
    c[:, C_MKEY:C_MQRY] = np.where(np.arange(S)[None, :] > tok[:, None], MASKED, 0)
    c[:, C_MQRY:C_NEG] = np.where(same & (tok[None, :] > tok[:, None]), MASKED, 0)
    c[:, C_NEG:C_DELTA] = -np.repeat(tok[:, None] == np.arange(S)[None, :], 2, axis=1).astype(np.float32)
    c[:, C_DELTA:C_HEAD] = tok[:, None] == np.arange(S)[None, :]
    c[:, C_HEAD:C_REV] = (p[:, None] % 32) // HD == np.arange(J)[None, :]
    c[:, C_REV:C_END] = E - np.arange(E)[None, :]
    return c


class Block:

    def __init__(self, i, off, rounds=1):
        self.i, self.off, self.rounds, self.par = i, off, rounds, off % 2

    def back(self, d):
        return Block(self.i, self.off - d, self.rounds)

    def exists(self):
        first, last = (0 <= n < NBLK for n in (self.off, self.off + 2 * (self.rounds - 1)))
        assert first == last
        return first

    def times(self, m, add=0):
        return m * self.off + add if self.i is None else self.i * (2 * m) + (m * self.off + add)

    def landed(self, per=16):
        h = self.off // 2
        return (h + 1) * per if self.i is None else self.i * per + (h + 1) * per


class Expert:

    def __init__(self, i, off, e, rounds):
        self.i, self.off, self.e, self.rounds = i, off, e, rounds

    def exists(self):
        first, last = (0 <= n < ROUNDS for n in (self.off, self.off + self.rounds - 1))
        assert first == last
        return first

    def times(self, m, add=0):
        return m * self.off + add if self.i is None else self.i * m + (m * self.off + add)

    def early(self, n):
        return self.i is None and E * self.off + self.e < n

    def count(self):
        return self.times(E, self.e + 1)


class Unit:

    def __init__(self, kind, blk, pair):
        self.kind, self.blk, self.pair = kind, blk, pair
        self.buf = pair
        self.col = pair * P

    def count(self):
        return self.blk.times(2, self.pair + 1)

    def tile(self):
        return self.blk.times(2, self.pair)


def settle(eng, done, n, sem, value):
    value = value if isinstance(value, int) else eng.snap(value)
    eng.wait_ge(done, n)
    eng.wait_ge(sem, value)


def unit_at(now, slot):
    now = now.back(-(slot // 4))
    slot %= 4
    blk = now if slot < 2 else now.back(LAG)
    return Unit(SELF if slot < 2 else CROSS, blk, slot % 2) if blk.exists() else None


def same_buffers(now, slot):
    return next((u for k in (2, 4) if (u := unit_at(now, slot - k))), None)


AHEAD = 6
FIRST, STEADY, LAST = -1, AHEAD + 2, NBLK - 3
END = NBLK + AHEAD + 1


def expert_at(now, slot):
    now = now.back(-(slot // 4))
    off = now.off - AHEAD
    x = Expert(now.i, off // 2, 4 * (off % 2) + slot % 4, now.rounds)
    return x if x.exists() else None


def keys_banks(now):
    return 5 if now.i is None and now.off < AHEAD else 0


def routed_at(now):
    x = expert_at(now.back(-1), 0)
    return x if x and x.e == 0 else None


def schedule(eng, time):
    for t in range(FIRST, STEADY):
        time(Block(None, t))
    rounds = (LAST + 1 - STEADY) // 2
    with eng.Fori(0, rounds) as i:
        time(Block(i, STEADY, rounds))
        time(Block(i, STEADY + 1, rounds))
    for t in range(STEADY + 2 * rounds, END + 1):
        time(Block(None, t))


def build(nc, x, ctx_in, cst, w, out):
    f32, f16, bf16 = mybir.dt.float32, mybir.dt.float16, mybir.dt.bfloat16
    ALU, ACT, AX = mybir.AluOpType, mybir.ActivationFunctionType, mybir.AxisListType
    st = ExitStack()

    def sb(name, shape, dt=f32):
        return st.enter_context(nc.sbuf_tensor(name, shape, dt))

    def sem(name):
        return st.enter_context(nc.semaphore(name))

    def two(name):
        return [sem(f"{name}_self"), sem(f"{name}_cross")]

    with st:
        consts = sb("consts", [P, C_END])
        ident = consts[:, C_ID:C_ONES]
        head_mask = consts[:, C_HEAD:C_REV]
        rev_idx = consts[:, C_REV:C_END]
        cbf = sb("consts_bf16", [P, C_HEAD], bf16)
        ident_bf, ones_bf = cbf[:, C_ID:C_ONES], cbf[:, C_ONES:C_MKEY]
        mask_key, mask_qry = cbf[:, C_MKEY:C_MQRY], cbf[:, C_MQRY:C_NEG]
        neg_delta, delta = cbf[:, C_NEG:C_DELTA], cbf[:, C_DELTA:C_HEAD]
        wq = [sb(f"wq{a}", [P, D]) for a in range(2)]
        wk = [sb(f"wk{a}", [P, D]) for a in range(2)]
        wv = [sb(f"wv{a}", [P, D]) for a in range(2)]
        wo = [sb(f"wo{a}", [P, D]) for a in range(2)]
        bq = [sb(f"bq{a}", [P, 1]) for a in range(2)]
        bk = [sb(f"bk{a}", [P, 1]) for a in range(2)]
        bv = [sb(f"bv{a}", [P, D]) for a in range(2)]
        bo = [sb(f"bo{a}", [P, D]) for a in range(2)]
        ln_g = [sb(f"ln_g{a}", [P, D]) for a in range(3)]
        ln_b = [sb(f"ln_b{a}", [P, D]) for a in range(3)]
        ln_gc = [sb(f"ln_gc{a}", [P, 1]) for a in range(2)]
        ln_bc = [sb(f"ln_bc{a}", [P, 1]) for a in range(2)]
        b1_bo = sb("b1_bo", [P, D])
        rw = sb("rw", [P, E])
        rb = sb("rb", [P, E])
        w1_hi, w1_lo = [sb(f"w1_{n}", [P, E, FF], f16) for n in ("hi", "lo")]
        w2 = sb("w2", [P, E, FC, D])
        b1_rows = sb("b1_rows", [E * FC, P])
        b1 = sb("b1", [P, E * FC])
        b2 = sb("b2", [E, D])

        tok_in = [[sb(f"tok_in{a}{p}", [P, PAIRS, D]) for p in range(2)] for a in range(2)]
        x_bo = [sb(f"x_bo{p}", [P, PAIRS, D]) for p in range(2)]
        inT = [[sb(f"inT{a}{p}", [P, BT]) for p in range(2)] for a in range(2)]
        x1T = [sb(f"x1T{p}", [P, BT]) for p in range(2)]
        x_rows = sb("x_rows", [P, TILES, D])
        x2T_hi, x2T_lo = [sb(f"x2T_{n}", [P, TOK], f16) for n in ("hi", "lo")]
        q_hl = [sb(f"q_hl{a}", [P, 2, BT], f16) for a in range(2)]
        k_hl = [sb(f"k_hl{a}", [P, 2, BT], f16) for a in range(2)]
        q_st = [[sb(f"q_st{a}{p}", [P, G, BT], f16) for p in range(2)] for a in range(2)]
        k_st = [sb(f"k_st{a}", [P, G, BT], f16) for a in range(2)]
        k_all = sb("k_all", [P, 4, G * J * BT], f16)
        k_one = [[k_all[:, 2 * a + p, :].rearrange("p (g j t) -> p g j t", g=G, j=J) for p in range(2)] for a in range(2)]
        v_f32 = [sb(f"v_f32{a}", [P, BT]) for a in range(2)]
        v_hi, v_lo = [[[sb(f"v_{n}{a}{p}", [P, PAIRS, 2, H, HD + 1], f16) for p in range(2)] for a in range(2)]
                      for n in ("hi", "lo")]
        row_max = [sb(f"row_max{p}", [P, H], bf16) for p in range(2)]
        max_diag = [sb(f"max_diag{p}", [P, HP, S, 2], bf16) for p in range(2)]
        probT = [sb(f"probT{p}", [P, H, S]) for p in range(2)]
        p_hi, p_lo = [[sb(f"prob_{n}{p}", [P, H, S], f16) for p in range(2)] for n in ("hi", "lo")]
        rden = [sb(f"rden{p}", [P, HP, 2]) for p in range(2)]
        o_n = [sb(f"o_n{p}", [P, 2, 2, HP, HD]) for p in range(2)]
        oT = [sb(f"oT{p}", [P, P]) for p in range(2)]
        res = [sb(f"res{p}", [P, D]) for p in range(2)]
        stats = [sb(f"stats{p}", [P, 6]) for p in range(2)]
        mv = [sb(f"mv{p}", [P, 2]) for p in range(2)]
        rstd = [sb(f"rstd{p}", [P, 1]) for p in range(2)]
        veps = [sb(f"veps{p}", [P, 1]) for p in range(2)]
        carrier = sb("carrier", [P, 1])
        eps = sb("eps", [P, MT])
        minus_half = sb("minus_half", [P, MT])
        yn = [sb(f"yn{p}", [P, D]) for p in range(2)]
        yg = [sb(f"yg{p}", [P, D]) for p in range(2)]

        x2_tile = [sb(f"x2_tile{p}", [P, P]) for p in range(2)]
        lg, prob, tmp, oh1, oh2, comb_new = [sb(n, [P, MT, E]) for n in ("lg", "prob", "tmp", "oh1", "oh2", "comb_new")]
        t1, m1, m2, cw1, cw2 = [sb(n, [P, MT]) for n in ("t1", "m1", "m2", "cw1", "cw2")]
        combT = sb("combT", [E, MB])
        comb = sb("comb", [P, MT, E])
        hid_all = sb("hid", [P, 2, FC, MB])
        hid = [hid_all[:, p, :, :] for p in range(2)]
        w1_in = hid_all[:, :, :, :].rearrange("p a c m -> p (a c m)").rearrange("p (e f) -> p e f", e=E)
        acc = sb("acc", [P, MT, D])
        fin = sb("fin", [P, MT, D])
        fst = sb("fst", [P, MT, 6])
        fmv = sb("fmv", [P, MT, 2])
        frs = sb("frs", [P, MT])
        bank = st.enter_context(nc.psum_tensor("bank", [P, 8, 512], f32))
        LG_COL = 36 * HP
        WO_COL = LG_COL + E
        SC, O_B, TURN, ROW, H_B, Y_B = 0, 2, 3, 4, 5, 7

        q_scr = [[nc.dram_tensor(f"q_scr{a}{p}", [2, P, BT], f16).ap() for p in range(2)] for a in range(2)]
        k_scr = [[nc.dram_tensor(f"k_scr{a}{p}", [2, P, BT], f16).ap() for p in range(2)] for a in range(2)]

        first_in, w_in, late_in = sem("first_weights_in"), sem("weights_in"), sem("late_weights_in")
        moe_in, w2_in = sem("w1_b1_b2_in"), sem("w2_in")
        cbf_ready = sem("consts_bf16_ready")
        zeroed, ZEROED = sem("constants_set"), 20
        b1_bo_ready = sem("ln1_b_plus_ca_bo")
        tok_landed = [[sem(f"tok_landed{a}{p}") for p in range(2)] for a in range(2)]
        xbo_ready = sem("x_bo_ready")
        inT_ready, inT_done = two("inT_ready"), two("inT_done")
        q_ready, k_ready = two("q_ready"), two("k_ready")
        q_hi, k_hi, q_lo, k_lo = two("q_hi"), two("k_hi"), two("q_lo"), two("k_lo")
        q_out, k_out = two("q_out"), two("k_out")
        q_back = [[sem(f"q_back{a}{p}") for p in range(2)] for a in range(2)]
        k_back = two("k_back")
        k_one_ready = two("k_one_ready")
        v_ready, v_done = two("v_ready"), two("v_done")
        s_ready, max_done, diag_ready = two("s_ready"), two("max_done"), two("diag_ready")
        st_ready, exp_done = two("st_ready"), two("exp_done")
        pv_ready, rden_done, on_ready = two("pv_ready"), two("rden_done"), two("on_ready")
        ot_ready, ot_done = two("ot_ready"), two("ot_done")
        wo_ready, res_done = two("wo_ready"), two("res_done")
        ve_done = two("veps_done")
        st_done, mv_done, rs_done, yn_ready = two("stats_done"), two("mv_done"), two("rstd_done"), two("yn_ready")
        yT_ready, yT_done = two("yT_ready"), two("yT_done")
        yg_done, x_done = two("yg_done"), two("x_done")
        w1_hi_ready, w1_lo_ready = sem("w1_hi_ready"), sem("w1_lo_ready")
        x2_lo_ready = sem("x2_lo_ready")
        v_hi_ready, v_sum = two("v_hi_ready"), two("v_sum")
        lo_first, lo_second = two("probs_lo_first_heads"), two("probs_lo_second_heads")
        x2_tile_ready = sem("x2_tile_ready")
        lg_ready, lg_done, route = sem("lg_ready"), sem("lg_done"), sem("route_step")
        e_ready, e_done, d_ready, d_done = sem("shifted"), sem("shifted_exp"), sem("second_less_first"), sem("its_exp")
        comb_ready, ct_ready, ct_done = sem("comb_ready"), sem("ct_ready"), sem("ct_done")
        b1_ready, b1_done = sem("b1_ready"), sem("b1_done")
        h_ready, h_done = sem("h_ready"), sem("h_done")
        y_ready, y_done = sem("y_ready"), sem("y_done")
        b2_ready, b2_done = sem("b2_ready"), sem("b2_done")
        f_stats, f_mv, f_veps, f_rstd = sem("f_stats"), sem("f_mv"), sem("f_veps"), sem("f_rstd")
        f_norm, f_gain, f_ready, f_out = sem("f_norm"), sem("f_gain"), sem("f_ready"), sem("f_out")

        blk = st.enter_context(nc.Block())
        FIRST_WEIGHTS, WEIGHTS, LATE_WEIGHTS = 7, 8, 16

        def tiles_of(v, x):
            n = x.times(MT)
            return v[:, n:n + MT, :] if x.i is None else v[:, bass.ds(n, MT), :]

        def heads_of_pairs(v):
            return v.rearrange("(p h d) n -> h p d n", h=2, d=HD)

        @blk.sync
        def _(sp):
            def wait(s, v):
                if not isinstance(v, int):
                    sp.compute_val(v)
                settle(sp, first_in, 16 * FIRST_WEIGHTS, s, v)

            def load_tokens(a, b):
                src = (x, ctx_in)[a]
                if not b.exists():
                    return
                if b.back(2).exists():
                    wait(inT_ready[a], b.back(2).times(1, 1))
                    if a == SELF:
                        wait(xbo_ready, b.back(2).times(1, 1))
                n = b.times(BT)
                rows = src[n:n + BT, :] if b.i is None else src[bass.ds(n, BT), :]
                sp.dma_start(tok_in[a][b.par][:, :, :], rows.rearrange("(t p) d -> p t d", p=P)).then_inc(
                    tok_landed[a][b.par], 16)

            def send(a, b, hi, lo, hl, scr, gone):
                wait(hi[a], b.times(1, 1))
                wait(lo[a], b.times(1, 1))
                sp.dma_start(scr[a][b.par].rearrange("s p t -> p s t"), hl[a][:, :, :]).then_inc(gone[a], 16)

            def fetch_q(a, b):
                if b.i is not None:
                    sp.compute_val(b.times(16, 16))
                    sp.compute_val(b.back(2).times(2, 2))
                wait(q_out[a], b.times(16, 16))
                if b.back(2).exists():
                    wait(st_ready[a], b.back(2).times(2, 2))
                for s in range(2):
                    for c in range(2):
                        r = 2 * s + c
                        sp.dma_start(q_st[a][b.par][32 * r:32 * r + 32, :, :],
                                     q_scr[a][b.par][s].rearrange("(g p) t -> p g t", g=G)).then_inc(
                                         q_back[a][b.par], 16)

            def fetch_k(a, b):
                if b.i is not None:
                    sp.compute_val(b.times(16, 16))
                    sp.compute_val(b.back(1).times(1, 1))
                wait(k_out[a], b.times(16, 16))
                if b.back(1).exists():
                    wait(k_one_ready[a], b.back(1).times(1, 1))
                for s in range(2):
                    for c in range(2):
                        r = s + 2 * c
                        sp.dma_start(k_st[a][32 * r:32 * r + 32, :, :],
                                     k_scr[a][b.par][s].rearrange("(g p) t -> p g t", g=G)).then_inc(k_back[a], 16)

            def load_late_weights():
                for dst, src in [(wo[CROSS][64 * h:64 * h + 64, :], heads_of_pairs(w["ca_wo"])[h]) for h in range(2)] + [
                        (v[:, :], w[name]) for v, name in (
                            (wq[CROSS], "ca_wq"), (wk[CROSS], "ca_wk"), (wv[CROSS], "ca_wv"), (rw, "router_w"))] + [
                        (v[:, :], w[name].partition_broadcast(P)) for v, name in (
                            (bv[CROSS], "ca_bv"), (ln_g[1], "ln2_g"), (ln_b[1], "ln2_b"), (ln_g[2], "ln3_g"),
                            (ln_b[2], "ln3_b"), (rb, "router_b"))] + [
                        (v[:, :], w[name].rearrange("(p a) -> p a", a=1)) for v, name in (
                            (bq[CROSS], "ca_bq"), (bk[CROSS], "ca_bk"), (ln_gc[1], "ln2_g"), (ln_bc[1], "ln2_b"))]:
                    sp.dma_start(dst, src).then_inc(late_in, 16)

            def time(now):
                sa, ca = now.back(-1), now.back(1)
                if now.i is None and now.off == 0:
                    load_late_weights()
                if now.i is None and now.off == 0:
                    for dst, src in ((w1_in, w["e_w1"].rearrange("e d f -> d e f")),
                                     (b1_rows[:, :], w["e_b1"].rearrange("e (c f) -> (e c) f", c=FC)),
                                     (b2[:, :], w["e_b2"])):
                        sp.dma_start(dst, src).then_inc(moe_in, 16)
                if now.i is None and now.off == 3:
                    sp.dma_start(w2[:, :, :, :], w["e_w2"].rearrange("e (c f) d -> f e c d", c=FC)).then_inc(w2_in, 16)
                if now.off >= 0:
                    load_tokens(SELF, now.back(-2))
                    load_tokens(CROSS, now.back(-1))
                if (x := expert_at(now, -5)) and x.e == E - 1:
                    wait(f_ready, x.times(1, 1))
                    n = x.times(MB)
                    rows = out[n:n + MB, :] if x.i is None else out[bass.ds(n, MB), :]
                    sp.dma_start(rows.rearrange("(t p) d -> p t d", p=P), fin[:, :, :]).then_inc(f_out, 16)
                if sa.exists():
                    send(SELF, sa, q_hi, q_lo, q_hl, q_scr, q_out)
                    send(SELF, sa, k_hi, k_lo, k_hl, k_scr, k_out)
                    fetch_q(SELF, sa)
                    fetch_k(SELF, sa)
                if ca.exists():
                    send(CROSS, ca, q_hi, q_lo, q_hl, q_scr, q_out)
                    fetch_q(CROSS, ca)
                    send(CROSS, ca, k_hi, k_lo, k_hl, k_scr, k_out)
                    fetch_k(CROSS, ca)

            load_tokens(SELF, Block(None, 0))
            for dst, src in ((consts, cst), (wq[SELF], w["sa_wq"]), (wk[SELF], w["sa_wk"]), (wv[SELF], w["sa_wv"]),
                             (bq[SELF], w["sa_bq"].rearrange("(p a) -> p a", a=1)),
                             (bk[SELF], w["sa_bk"].rearrange("(p a) -> p a", a=1)),
                             (bv[SELF], w["sa_bv"].partition_broadcast(P))):
                sp.dma_start(dst[:, :], src).then_inc(first_in, 16)
            load_tokens(SELF, Block(None, 1))
            load_tokens(CROSS, Block(None, 0))
            schedule(sp, time)

            sp.wait_ge(f_out, 16 * ROUNDS)

        @blk.gpsimd
        def _(pool):
            for a in range(2):
                for p in range(2):
                    pool.memset(v_hi[a][p][:, :, :, :, :], 0.0).then_inc(zeroed, 1)
                    pool.memset(v_lo[a][p][:, :, :, :, :], 0.0).then_inc(zeroed, 1)
            for p in range(2):
                pool.memset(o_n[p][:, :, :, :, :], 0.0).then_inc(zeroed, 1)
            pool.memset(minus_half[:, :], -0.5).then_inc(zeroed, 1)
            pool.memset(eps[:, :], EPS).then_inc(zeroed, 1)
            pool.wait_ge(zeroed, 12)
            for a in range(2):
                for p in range(2):
                    for b in range(2):
                        pool.memset(v_hi[a][p][64 * b:64 * b + 64, :, b, :, HD:HD + 1], 1.0).then_inc(zeroed, 1)
                        pool.wait_ge(zeroed, 12 + 4 * a + 2 * p + b + 1)
            for dst, src in [(wo[SELF][64 * h:64 * h + 64, :], heads_of_pairs(w["sa_wo"])[h]) for h in range(2)] + [
                    (v[:, :], w[name].partition_broadcast(P)) for v, name in (
                        (bo[SELF], "sa_bo"), (bo[CROSS], "ca_bo"), (ln_g[0], "ln1_g"), (ln_b[0], "ln1_b"))] + [
                    (v[:, :], w[name].rearrange("(p a) -> p a", a=1)) for v, name in ((ln_gc[0], "ln1_g"), (ln_bc[0], "ln1_b"))]:
                pool.dma_start(dst, src).then_inc(w_in, 16)
            pool.wait_ge(w_in, 16 * WEIGHTS)
            pool.tensor_tensor(b1_bo[:, :], ln_b[0][:, :], bo[CROSS][:, :], ALU.add).then_inc(b1_bo_ready, 1)
            pool.wait_ge(b1_bo_ready, 1)

            def add_bo(b):
                pool.wait_ge(tok_landed[SELF][b.par], b.landed())
                if b.back(2).exists():
                    pool.wait_ge(res_done[SELF], b.back(2).times(2, 2))
                pool.tensor_tensor(x_bo[b.par][:, :, :], tok_in[SELF][b.par][:, :, :],
                                   bo[SELF][:, :].unsqueeze(1).to_broadcast([P, PAIRS, D]), ALU.add).then_inc(xbo_ready, 1)

            def spread(u):
                a, n = u.kind, u.buf
                pool.wait_ge(mv_done[a], u.count())
                pool.tensor_tensor(veps[n][:, :], mv[n][:, 1:2], eps[:, 0:1], ALU.add).then_inc(ve_done[a], 1)
                pool.wait_ge(ve_done[a], u.count())
                pool.tensor_tensor(rstd[n][:, :], veps[n][:, :], minus_half[:, 0:1], ALU.pow).then_inc(rs_done[a], 1)

            def gain(u):
                a = u.kind
                pool.wait_ge(yn_ready[a], u.count())
                pool.tensor_tensor(yg[u.buf][:, :], yn[u.buf][:, :], ln_g[a][:, :], ALU.mult).then_inc(yg_done[a], 1)
                pool.wait_ge(yg_done[a], u.count())
                dst = x_rows[:, u.tile(), :]
                off = (b1_bo, ln_b[1])[a]
                pool.tensor_tensor(dst, yg[u.buf][:, :], off[:, :], ALU.add).then_inc(x_done[a], 1)

            def x2_low(u):
                pool.wait_ge(yT_done[CROSS], u.count())
                pool.wait_ge(x2_tile_ready, u.count())
                n = u.blk.times(BT, u.col)
                hi, lo = [v[:, n:n + P] if u.blk.i is None else v[:, bass.ds(n, P)] for v in (x2T_hi, x2T_lo)]
                pool.tensor_tensor(lo, x2_tile[u.buf][:, :], hi, ALU.subtract).then_inc(x2_lo_ready, 1)

            def probs_low(u):
                pool.wait_ge(exp_done[u.kind], u.count())
                h = slice(DVE_HEADS, H)
                pool.tensor_tensor(p_lo[u.buf][:, h, :], probT[u.buf][:, h, :], p_hi[u.buf][:, h, :], ALU.subtract).then_inc(
                    lo_second[u.kind], 1)

            def last_spread(x):
                pool.wait_ge(f_mv, x.times(1, 1))
                pool.tensor_tensor(frs[:, :], fmv[:, :, 1], eps[:, :], ALU.add).then_inc(f_veps, 1)
                pool.wait_ge(f_veps, x.times(1, 1))
                pool.tensor_tensor(frs[:, :], frs[:, :], minus_half[:, :], ALU.pow).then_inc(f_rstd, 1)

            def last_gain(x):
                pool.wait_ge(f_norm, x.times(1, 1))
                pool.tensor_tensor(fin[:, :, :], fin[:, :, :], ln_g[2][:, :].unsqueeze(1).to_broadcast([P, MT, D]),
                                   ALU.mult).then_inc(f_gain, 1)
                pool.wait_ge(f_gain, x.times(1, 1))
                pool.tensor_tensor(fin[:, :, :], fin[:, :, :], ln_b[2][:, :].unsqueeze(1).to_broadcast([P, MT, D]),
                                   ALU.add).then_inc(f_ready, 1)

            def time(now):
                if now.off == 1:
                    pool.wait_ge(late_in, 16 * LATE_WEIGHTS)
                for s in range(4):
                    if s == 0 and now.back(-1).exists():
                        add_bo(now.back(-1))
                    if u := unit_at(now, s - 3):
                        spread(u)
                    if u := unit_at(now, s - 4):
                        gain(u)
                    if (u := unit_at(now, s - 4)) and u.kind == CROSS:
                        x2_low(u)
                    if u := unit_at(now, s - 1):
                        probs_low(u)
                    if (x := expert_at(now, s - 1)) and x.e == E - 1:
                        last_spread(x)
                    if (x := expert_at(now, s - 2)) and x.e == E - 1:
                        last_gain(x)

            schedule(pool, time)

        @blk.scalar
        def _(act):
            act.wait_ge(first_in, 16 * FIRST_WEIGHTS)

            def turned(a, b):
                act.wait_ge(inT_ready[a], b.times(1, 1))
                if b.back(2).exists():
                    act.wait_ge(v_ready[a], b.back(2).times(1, 1))
                act.activation(inT[a][b.par][:, :], bank[:, TURN, a * BT:(a + 1) * BT], ACT.Copy).then_inc(inT_done[a], 1)

            def high(a, b, ready, hi, hl, bias, gone, half=0):
                act.wait_ge(ready[a], b.times(1, 1))
                if b.back(1).exists():
                    act.wait_ge(gone[a], b.times(16))
                act.activation(hl[a][:, 0, :], bank[:, ROW, half * BT:(half + 1) * BT], ACT.Identity, bias=bias[a][:, :]).then_inc(hi[a], 1)

            def exps(now, u, v):
                a = u.kind
                act.wait_ge(st_ready[a], u.count())
                if v:
                    act.wait_ge(pv_ready[v.kind], v.count())
                kb = keys_banks(now)
                act.activation(probT[u.buf][:, :, :].rearrange("p h q -> p (h q)"),
                               bank[:, kb:kb + 2, :].rearrange("p a n -> p (a n)"), ACT.Exp,
                               scale=float(HD) ** -0.5)
                act.activation(p_hi[u.buf][:, :, :].rearrange("p h q -> p (h q)"),
                               bank[:, kb:kb + 2, :].rearrange("p a n -> p (a n)"), ACT.Exp,
                               scale=float(HD) ** -0.5).then_inc(exp_done[a], 1)

            def o_turned(u, v):
                a = u.kind
                act.wait_ge(ot_ready[a], u.count())
                if v:
                    act.wait_ge(wo_ready[v.kind], v.count())
                act.activation(oT[u.buf][:, :], bank[:, TURN, 0:P], ACT.Copy).then_inc(ot_done[a], 1)

            def y_turned(u):
                a, b = u.kind, u.blk
                act.wait_ge(yT_ready[a], u.count())
                if a == SELF:
                    if b.back(2).exists():
                        act.wait_ge(q_ready[CROSS], b.back(2).times(1, 1))
                    act.activation(x1T[b.par][:, u.col:u.col + P], bank[:, TURN, 0:P], ACT.Identity,
                                   bias=ln_bc[a][:, :], scale=ln_gc[a][:, :]).then_inc(yT_done[a], 1)
                    return
                if b.back(1).exists():
                    act.wait_ge(lg_ready, Unit(CROSS, b.back(1), u.pair).count())
                    act.wait_ge(x2_lo_ready, Unit(CROSS, b.back(1), u.pair).count())
                act.activation(x2_tile[u.buf][:, :], bank[:, TURN, 0:P], ACT.Identity,
                               bias=ln_bc[a][:, :], scale=ln_gc[a][:, :]).then_inc(x2_tile_ready, 1)
                n = b.times(BT, u.col)
                act.activation(x2T_hi[:, n:n + P] if b.i is None else x2T_hi[:, bass.ds(n, P)], bank[:, TURN, 0:P],
                               ACT.Identity, bias=ln_bc[a][:, :], scale=ln_gc[a][:, :]).then_inc(yT_done[a], 1)

            def gelus(x, chunks):
                for c in chunks:
                    k = x.e * FC + c
                    act.wait_ge(h_ready, x.times(E * FC, k + 1))
                    if c == 0 and not x.early(2):
                        act.wait_ge(y_ready, x.times(E, x.e - 1))
                    act.activation(hid[x.e % 2][:, c, :], bank[:, H_B + c % 2, :], ACT.Gelu,
                                   bias=b1[:, k:k + 1], scale=1 / W1_SCALE).then_inc(h_done, 1)

            def time(now):
                sa, ca = now.back(-1), now.back(1)
                r = routed_at(now)
                for s in range(4):
                    x = expert_at(now, s)
                    if now.i is None and now.off in W1_TIMES:
                        e = 4 * (now.off - W1_TIMES[0]) + s
                        act.wait_ge(moe_in, 48)
                        act.activation(w1_hi[:, e, :], w1_in[:, e, :], ACT.Copy, scale=W1_SCALE).then_inc(w1_hi_ready, 1)
                    if s == 0 and now.i is None and now.off == AHEAD - 1:
                        act.wait_ge(b1_ready, 1)
                        act.activation(b1[:, :], bank[:, Y_B, 0:E * FC], ACT.Copy).then_inc(b1_done, 1)
                        act.wait_ge(b1_done, 1)
                    if now.off == 0 and s == 2:
                        act.wait_ge(w_in, 16 * WEIGHTS)
                    if now.off == 1 and s == 0:
                        act.wait_ge(late_in, 16 * LATE_WEIGHTS)
                    if u := unit_at(now, s - 3):
                        o_turned(u, same_buffers(now, s - 3))
                    if x:
                        if x.early(1):
                            act.wait_ge(w1_lo_ready, E)
                        gelus(x, (0, 1, 2, 3))
                    if u := unit_at(now, s - 4):
                        y_turned(u)
                    if s == 0:
                        if ca.exists():
                            act.wait_ge(inT_ready[CROSS], ca.times(1, 1))
                        if sa.exists():
                            turned(SELF, sa)
                        if ca.exists():
                            turned(CROSS, ca)
                    if u := unit_at(now, s - 1):
                        exps(now, u, same_buffers(now, s - 1))
                    if s == 1 and sa.exists():
                        act.wait_ge(k_ready[SELF], sa.times(1, 1))
                        high(SELF, sa, q_ready, q_hi, q_hl, bq, q_out)
                        high(SELF, sa, k_ready, k_hi, k_hl, bk, k_out, 1)
                    if s == 2 and ca.exists():
                        if sa.exists():
                            act.wait_ge(v_ready[SELF], sa.times(1, 1))
                        high(CROSS, ca, q_ready, q_hi, q_hl, bq, q_out)
                    if s == 3 and ca.exists():
                        act.wait_ge(v_ready[CROSS], ca.times(1, 1))
                        high(CROSS, ca, k_ready, k_hi, k_hl, bk, k_out)
                    if r and s == 1:
                        act.wait_ge(e_ready, r.times(1, 1))
                        act.activation(tmp[:, :, :], lg[:, :, :], ACT.Exp).then_inc(e_done, 1)
                    if r and s == 2:
                        act.wait_ge(d_ready, r.times(1, 1))
                        act.activation(t1[:, :], m2[:, :], ACT.Exp).then_inc(d_done, 1)
                    if r and s == 3:
                        act.wait_ge(ct_ready, r.times(1, 1))
                        act.activation(combT[:, :], bank[0:E, TURN, :], ACT.Copy).then_inc(ct_done, 1)

            schedule(act, time)

        @blk.vector
        def _(dve):
            dve.wait_ge(first_in, 16 * FIRST_WEIGHTS)
            dve.tensor_copy(cbf[:, :], consts[:, 0:C_HEAD]).then_inc(cbf_ready, 1)
            dve.wait_ge(cbf_ready, 1)

            def low(a, b, hi, lo, hl, bias, half=0):
                dve.wait_ge(hi[a], b.times(1, 1))
                dve.scalar_tensor_tensor(hl[a][:, 1, :], bank[:, ROW, half * BT:(half + 1) * BT], bias[a][:, :], hl[a][:, 0, :],
                                         ALU.add, ALU.subtract).then_inc(lo[a], 1)

            def masks(a, b):
                dve.wait_ge(k_back[a], b.times(64, 64))
                if b.back(2).exists():
                    dve.wait_ge(st_ready[a], b.back(2).times(2, 2))
                for j in range(J):
                    last = dve.tensor_scalar(k_one[a][b.par][:, :, j, :], k_st[a][:, :, :],
                                             head_mask[:, j:j + 1], None, ALU.mult)
                last.then_inc(k_one_ready[a], 1)

            def v_rows(a, b):
                dve.wait_ge(v_ready[a], b.times(1, 1))
                if b.back(2).exists():
                    dve.wait_ge(pv_ready[a], b.back(2).times(2, 2))
                dve.tensor_tensor(v_f32[a][:, :].rearrange("p (t d) -> p t d", t=PAIRS),
                                  bank[:, ROW, BT:2 * BT].rearrange("p (t d) -> p t d", t=PAIRS),
                                  bv[a][:, :].unsqueeze(1).to_broadcast([P, PAIRS, D]), ALU.add).then_inc(v_sum[a], 1)
                dve.wait_ge(v_sum[a], b.times(1, 1))
                v = v_f32[a][:, :].rearrange("p (t h d) -> p t h d", t=PAIRS, h=H)
                hi, lo = v_hi[a][b.par], v_lo[a][b.par]
                for h in range(2):
                    r = slice(64 * h, 64 * h + 64)
                    last = dve.tensor_copy(hi[r, :, h, :, 0:HD], v[r, :, :, :])
                last.then_inc(v_hi_ready[a], 1)
                dve.wait_ge(v_hi_ready[a], b.times(1, 1))
                for h in range(2):
                    r = slice(64 * h, 64 * h + 64)
                    last = dve.tensor_tensor(lo[r, :, h, :, 0:HD], v[r, :, :, :], hi[r, :, h, :, 0:HD], ALU.subtract)
                last.then_inc(v_done[a], 1)

            def probs_low(u):
                dve.wait_ge(exp_done[u.kind], u.count())
                h = slice(0, DVE_HEADS)
                dve.tensor_tensor(p_lo[u.buf][:, h, :], probT[u.buf][:, h, :], p_hi[u.buf][:, h, :], ALU.subtract).then_inc(
                    lo_first[u.kind], 1)

            def maxima(u):
                a = u.kind
                dve.wait_ge(s_ready[a], u.count())
                dve.reduce_max(row_max[u.buf][:, :],
                               bank[:, SC:SC + 2, :].rearrange("p a (h k) -> p (a h) k", k=S), AX.X).then_inc(max_done[a], 1)
                dve.wait_ge(max_done[a], u.count())
                m = row_max[u.buf][:, :].rearrange("p (a c) -> p a c", c=2).unsqueeze(2).to_broadcast([P, HP, S, 2])
                dl = neg_delta.rearrange("p (q c) -> p q c", c=2).unsqueeze(1).to_broadcast([P, HP, S, 2])
                dve.tensor_tensor(max_diag[u.buf][:, :, :, :], dl, m, ALU.mult).then_inc(diag_ready[a], 1)

            def outputs(u):
                a = u.kind
                dve.wait_ge(pv_ready[a], u.count())
                o = bank[:, O_B, 0:HP * 36].rearrange("p (a b c d) -> p a b c d", a=HP, b=2, c=2)
                for h in range(2):
                    r = slice(64 * h, 64 * h + 64)
                    last = dve.reciprocal(rden[u.buf][r, :, :], o[r, :, :, h, HD])
                last.then_inc(rden_done[a], 1)
                dve.wait_ge(rden_done[a], u.count())
                for h in range(2):
                    r = slice(64 * h, 64 * h + 64)
                    last = dve.tensor_tensor(o_n[u.buf][r, :, h, :, :].rearrange("p b a d -> p a b d"), o[r, :, :, h, 0:HD],
                                             rden[u.buf][r, :, :].unsqueeze(3).to_broadcast([64, HP, 2, HD]), ALU.mult)
                last.then_inc(on_ready[a], 1)

            def residual(u):
                a, n = u.kind, u.buf
                dve.wait_ge(wo_ready[a], u.count())
                if a == SELF:
                    dve.wait_ge(xbo_ready, u.blk.times(1, 1))
                    r = x_bo[u.blk.par][:, u.pair, :]
                else:
                    dve.wait_ge(x_done[SELF], u.count())
                    r = x_rows[:, u.tile(), :]
                dve.tensor_tensor(res[n][:, :], bank[:, O_B, WO_COL:WO_COL + D], r, ALU.add).then_inc(res_done[a], 1)
                dve.wait_ge(res_done[a], u.count())
                dve.bn_stats(stats[n][:, :], res[n][:, :]).then_inc(st_done[a], 1)
                dve.wait_ge(st_done[a], u.count())
                dve.tensor_copy(carrier[:, :], consts[:, 0:1])
                dve.bn_aggr(mv[n][:, :], stats[n][:, :]).then_inc(mv_done[a], 1)

            def norm(u, v):
                a, n = u.kind, u.buf
                dve.wait_ge(rs_done[a], u.count())
                if v:
                    dve.wait_ge(yT_ready[v.kind], v.count())
                    dve.wait_ge(yg_done[v.kind], v.count())
                dve.tensor_scalar(yn[n][:, :], res[n][:, :], mv[n][:, 0:1], rstd[n][:, :], ALU.subtract,
                                  ALU.mult).then_inc(yn_ready[a], 1)

            def wide(v):
                return v[:, :].unsqueeze(2).to_broadcast([P, MT, E])

            class Steps:

                def __init__(self, x, done):
                    self.x, self.done = x, done

                def __call__(self, ins):
                    self.done += 1
                    ins.then_inc(route, 1)
                    dve.wait_ge(route, self.x.times(ROUTE_STEPS, self.done))

            def logits(u):
                dve.wait_ge(lg_ready, u.count())
                dve.tensor_tensor(lg[:, 2 * u.blk.par + u.pair, :], bank[:, O_B, LG_COL:LG_COL + E], rb[:, :], ALU.add).then_inc(lg_done, 1)

            def route_logits(x):
                step = Steps(x, 0)
                dve.wait_ge(lg_done, x.times(MT, MT))
                step(dve.reduce_max(t1[:, :], lg[:, :, :], AX.X))
                dve.tensor_tensor(lg[:, :, :], lg[:, :, :], wide(t1), ALU.subtract).then_inc(e_ready, 1)

            def first_of(step, m):
                step(dve.reduce_max(m[:, :], prob[:, :, :], AX.X))
                step(dve.tensor_tensor(tmp[:, :, :], prob[:, :, :], wide(m), ALU.is_equal))
                step(dve.tensor_tensor(tmp[:, :, :], tmp[:, :, :],
                                       rev_idx.unsqueeze(1).to_broadcast([P, MT, E]), ALU.mult))
                step(dve.reduce_max(t1[:, :], tmp[:, :, :], AX.X))

            def route_probs(x):
                step = Steps(x, 1)
                dve.wait_ge(e_done, x.times(1, 1))
                step(dve.reduce_sum(t1[:, :], tmp[:, :, :], AX.X))
                step(dve.reciprocal(t1[:, :], t1[:, :]))
                step(dve.tensor_tensor(prob[:, :, :], tmp[:, :, :], wide(t1), ALU.mult))
                first_of(step, m1)
                step(dve.tensor_tensor(oh1[:, :, :], tmp[:, :, :], wide(t1), ALU.is_equal))
                step(dve.scalar_tensor_tensor(prob[:, :, :].rearrange("p t e -> p (t e)"),
                                              oh1[:, :, :].rearrange("p t e -> p (t e)"), -2.0,
                                              prob[:, :, :].rearrange("p t e -> p (t e)"), ALU.mult, ALU.add))
                first_of(step, m2)
                step(dve.tensor_tensor(oh2[:, :, :], tmp[:, :, :], wide(t1), ALU.is_equal))
                dve.tensor_tensor(m2[:, :], m2[:, :], m1[:, :], ALU.subtract).then_inc(d_ready, 1)

            def route_weights(x):
                step = Steps(x, 15)
                dve.wait_ge(d_done, x.times(1, 1))
                step(dve.tensor_scalar(cw1[:, :], t1[:, :], 1.0, None, ALU.add))
                step(dve.reciprocal(cw1[:, :], cw1[:, :]))
                step(dve.tensor_tensor(cw2[:, :], t1[:, :], cw1[:, :], ALU.mult))
                step(dve.tensor_tensor(oh1[:, :, :], oh1[:, :, :], wide(cw1), ALU.mult))
                step(dve.tensor_tensor(oh2[:, :, :], oh2[:, :, :], wide(cw2), ALU.mult))
                step(dve.tensor_tensor(comb_new[:, :, :], oh1[:, :, :], oh2[:, :, :], ALU.add))

            def add_b2(x):
                dve.wait_ge(x_done[CROSS], x.times(MT, MT))
                dve.wait_ge(b2_ready, x.times(1, 1))
                dve.tensor_tensor(tiles_of(x_rows, x), tiles_of(x_rows, x), bank[:, Y_B, :].rearrange("p (t d) -> p t d", t=MT),
                                  ALU.add).then_inc(b2_done, 1)

            def combine(x):
                if x.e == 0:
                    dve.tensor_copy(comb[:, :, :], comb_new[:, :, :]).then_inc(comb_ready, 1)
                    dve.wait_ge(b2_done, x.times(1, 1))
                    dve.wait_ge(comb_ready, x.times(1, 1))
                    if not x.early(1):
                        dve.wait_ge(f_norm, x.times(1))
                else:
                    dve.wait_ge(y_done, x.times(E, x.e))
                dve.wait_ge(y_ready, x.count())
                n = x.times(MT)
                for t in range(MT):
                    last = dve.scalar_tensor_tensor(acc[:, t, :], bank[:, Y_B, t * D:(t + 1) * D], comb[:, t, x.e:x.e + 1],
                                                    acc[:, t, :] if x.e else x_rows[:, n + t, :], ALU.mult, ALU.add)
                last.then_inc(y_done, 1)

            def last_stats(x):
                dve.wait_ge(y_done, x.count())
                for t in range(MT):
                    last = dve.bn_stats(fst[:, t, :], acc[:, t, :])
                last.then_inc(f_stats, 1)
                dve.wait_ge(f_stats, x.times(1, 1))
                dve.tensor_copy(carrier[:, :], consts[:, 0:1])
                for t in range(MT):
                    last = dve.bn_aggr(fmv[:, t, :], fst[:, t, :])
                last.then_inc(f_mv, 1)

            def last_norm(x):
                dve.wait_ge(f_rstd, x.times(1, 1))
                if not x.early(E):
                    dve.wait_ge(f_out, x.times(16))
                for t in range(MT):
                    last = dve.tensor_scalar(fin[:, t, :], acc[:, t, :], fmv[:, t, 0:1], frs[:, t:t + 1], ALU.subtract,
                                             ALU.mult)
                last.then_inc(f_norm, 1)

            def time(now):
                sa, ca = now.back(-1), now.back(1)
                r = routed_at(now)
                for s in range(4):
                    x, y = expert_at(now, s - 1), expert_at(now, s - 2)
                    if now.off == FIRST and s == 2:
                        dve.wait_ge(zeroed, ZEROED)
                    if now.off == 0 and s == 2:
                        dve.wait_ge(w_in, 16 * WEIGHTS)
                    if now.off == 1 and s == 0:
                        dve.wait_ge(late_in, 16 * LATE_WEIGHTS)
                    if now.i is None and now.off in W1_TIMES:
                        e = 4 * (now.off - W1_TIMES[0]) + s
                        dve.wait_ge(w1_hi_ready, e + 1)
                        dve.scalar_tensor_tensor(w1_lo[:, e, :], w1_in[:, e, :], W1_SCALE, w1_hi[:, e, :], ALU.mult,
                                                 ALU.subtract).then_inc(w1_lo_ready, 1)
                    if u := unit_at(now, s):
                        maxima(u)
                    if u := unit_at(now, s - 2):
                        dve.wait_ge(pv_ready[u.kind], u.count())
                    if u := unit_at(now, s - 3):
                        dve.wait_ge(wo_ready[u.kind], u.count())
                    if (u := unit_at(now, s - 5)) and u.kind == CROSS:
                        logits(u)
                    if u := unit_at(now, s - 2):
                        outputs(u)
                    if u := unit_at(now, s - 3):
                        residual(u)
                    if s == 1 and ca.back(1).exists():
                        masks(CROSS, ca.back(1))
                    if s == 3 and sa.exists():
                        masks(SELF, sa)
                    if s == 0 and (q := expert_at(now, 0)) and q.e == 0:
                        add_b2(q)
                    if y and y.e == E - 1:
                        last_norm(y)
                    if r and s == 2:
                        route_weights(r)
                    if u := unit_at(now, s - 3):
                        norm(u, same_buffers(now, s - 3))
                    if u := unit_at(now, s - 1):
                        probs_low(u)
                    if s == 1 and sa.exists():
                        dve.wait_ge(k_hi[SELF], sa.times(1, 1))
                        low(SELF, sa, q_hi, q_lo, q_hl, bq)
                        low(SELF, sa, k_hi, k_lo, k_hl, bk, 1)
                    if s == 2 and ca.exists():
                        low(CROSS, ca, q_hi, q_lo, q_hl, bq)
                    if s == 3 and ca.exists():
                        low(CROSS, ca, k_hi, k_lo, k_hl, bk)
                    if s == 2 and sa.exists():
                        v_rows(SELF, sa)
                    if s == 3 and ca.exists():
                        v_rows(CROSS, ca)
                    if x:
                        combine(x)
                        if x.e == E - 1:
                            last_stats(x)
                    if r and s == 0:
                        route_logits(r)
                    if r and s == 1:
                        route_probs(r)

            schedule(dve, time)

        @blk.tensor
        def _(pe):
            pe.wait_ge(cbf_ready, 1)

            def after(now, s, part, parts, reader):
                order = [(q, k) for q in range(s - 8, s + 1) for k in parts]
                for q, k in reversed(order[:order.index((s, part))]):
                    if found := reader(now.back(-(q // 4)), q, q % 4, k):
                        pe.wait_ge(*found)
                        return

            def turn_free(now, s, part):
                def reader(t, q, r, k):
                    if k == "o" and (u := unit_at(now, q - 3)):
                        return ot_done[u.kind], u.count()
                    if k == "y" and (u := unit_at(now, q - 4)):
                        return yT_done[u.kind], u.count()
                    if k == "inputs" and r == 0 and t.back(1).exists():
                        return inT_done[CROSS], t.back(1).times(1, 1)
                    if k == "inputs" and r == 0 and t.back(-1).exists():
                        return inT_done[SELF], t.back(-1).times(1, 1)
                    if k == "comb" and r == 3 and (x := routed_at(t)):
                        return ct_done, x.times(1, 1)
                after(now, s, part, ("o", "y", "inputs", "comb"), reader)

            def row_free(now, s):
                def reader(t, q, r, k):
                    sa, ca = t.back(-1), t.back(1)
                    if r == 1 and sa.exists():
                        return k_lo[SELF], sa.times(1, 1)
                    if r == 2 and sa.exists():
                        return v_sum[SELF], sa.times(1, 1)
                    if r == 2 and ca.exists():
                        return q_lo[CROSS], ca.times(1, 1)
                    if r == 3 and ca.exists():
                        return v_sum[CROSS], ca.times(1, 1)
                after(now, s, "prepared", ("prepared",), reader)

            def outs_free(now, s):
                def reader(t, q, r, k):
                    if u := unit_at(now, q - 3):
                        return res_done[u.kind], u.count()
                    if u := unit_at(now, q - 2):
                        return on_ready[u.kind], u.count()
                    if (u := unit_at(now, q - 5)) and u.kind == CROSS:
                        return lg_done, u.count()
                after(now, s, "both", ("both",), reader)

            def scores_free(now, s, part):
                place = keys_banks(now) if part == "keys" else SC

                def reader(t, q, r, k):
                    if k == "queries" and place == SC and (u := unit_at(now, q)):
                        return max_done[u.kind], u.count()
                    if k == "keys" and place == keys_banks(t) and (u := unit_at(now, q - 1)):
                        return exp_done[u.kind], u.count()
                after(now, s, part, ("queries", "keys"), reader)

            def sums_free(now, s, part):
                def reader(t, q, r, k):
                    if k == "down" and (x := expert_at(now, q - 1)):
                        return y_done, x.count()
                    if k == "b2" and r == 0 and (x := expert_at(t, 0)) and x.e == 0:
                        return b2_done, x.times(1, 1)
                after(now, s, part, ("b2", "down"), reader)

            def turn_in(a, b):
                pe.wait_ge(tok_landed[a][b.par], b.landed())
                for t in range(PAIRS):
                    last = pe.transpose(bank[:, TURN, a * BT + t * P:a * BT + (t + 1) * P], tok_in[a][b.par][:, t, :], ident)
                last.then_inc(inT_ready[a], 1)

            def project(wt, src, ready, a, half=0):
                pe.matmul(bank[:, ROW, half * BT:(half + 1) * BT], wt[a][:, :], src[:, :], start=True, stop=True).then_inc(ready[a], 1)

            def v_proj(a, b):
                for t in range(PAIRS):
                    last = pe.matmul(bank[:, ROW, BT + t * P:BT + (t + 1) * P], inT[a][b.par][:, t * P:(t + 1) * P], wv[a][:, :],
                                     start=True, stop=True)
                last.then_inc(v_ready[a], 1)

            def scores(now, s, u):
                a, b = u.kind, u.blk
                pe.wait_ge(q_back[a][b.par], b.landed(64))
                pe.wait_ge(k_one_ready[a], b.times(1, 1))
                scores_free(now, s, "queries")
                q, k = q_st[a][b.par], k_one[a][b.par]
                for n in range(2):
                    if a == SELF:
                        pe.matmul(bank[:, SC + n, :], ident_bf, mask_key.unsqueeze(1).to_broadcast([P, H // 2, S]),
                                  start=True, stop=True)
                    for gi in range(2):
                        for h in range(2):
                            c = u.col + 64 * h
                            last = pe.matmul(bank[64 * h:64 * h + 64, SC + n, 256 * gi:256 * gi + 256],
                                             q[:, 2 * n + gi, c:c + 64], k[:, 2 * n + gi, :, c:c + 64],
                                             start=a == CROSS and gi == 0, stop=True, skip_group_check=True)
                last.then_inc(s_ready[a], 1)

            def scores_T(now, s, u):
                a, b = u.kind, u.blk
                pe.wait_ge(diag_ready[a], u.count())
                scores_free(now, s, "keys")
                kb = keys_banks(now)
                q, k = q_st[a][b.par], k_one[a][b.par]
                for n in range(2):
                    pe.matmul(bank[:, kb + n, :], ones_bf,
                              max_diag[u.buf][:, 4 * n:4 * n + 4, :, :].rearrange("p a q c -> p a c q"),
                              start=True, stop=True)
                    if a == SELF:
                        pe.matmul(bank[:, kb + n, :], mask_qry, delta.unsqueeze(1).to_broadcast([P, H // 2, S]),
                                  start=False, stop=True, skip_group_check=True)
                    for hh in range(H // 2):
                        g, j = divmod(8 * n + hh, J)
                        for h in range(2):
                            c = u.col + 64 * h
                            last = pe.matmul(bank[64 * h:64 * h + 64, kb + n, 64 * hh:64 * hh + 64],
                                             k[:, g, j, c:c + 64], q[:, g, c:c + 64],
                                             start=False, stop=True, skip_group_check=True)
                last.then_inc(st_ready[a], 1)

            def weigh(u):
                a, b = u.kind, u.blk
                pe.wait_ge(lo_first[a], u.count())
                pe.wait_ge(lo_second[a], u.count())
                pe.wait_ge(v_done[a], b.times(1, 1))
                for p in range(HP):
                    ph, pl = [v[u.buf][:, 2 * p:2 * p + 2, :].rearrange("p h q -> p (h q)") for v in (p_hi, p_lo)]
                    vh, vl = [v[a][b.par][:, u.pair, :, 2 * p:2 * p + 2, :].rearrange("p b h d -> p b (h d)")
                              for v in (v_hi, v_lo)]
                    for k, (pt, v) in enumerate(((ph, vh), (ph, vl), (pl, vh))):
                        last = pe.matmul(bank[:, O_B, 36 * p:36 * p + 36], pt, v, start=k == 0, stop=k == 2,
                                         skip_group_check=True)
                last.then_inc(pv_ready[a], 1)

            def turn_o(now, s, u):
                turn_free(now, s, "o")
                pe.wait_ge(on_ready[u.kind], u.count())
                for b in range(2):
                    last = pe.matmul(bank[:, TURN, 64 * b:64 * b + 64],
                                     o_n[u.buf][:, b, :, :, :].rearrange("p c a d -> p (c a d)"),
                                     consts[:, C_DELTA:C_HEAD], start=True, stop=True)
                last.then_inc(ot_ready[u.kind], 1)

            def out_proj(u):
                pe.wait_ge(ot_done[u.kind], u.count())
                pe.matmul(bank[:, O_B, WO_COL:WO_COL + D], oT[u.buf][:, :], wo[u.kind][:, :], start=True, stop=True).then_inc(
                    wo_ready[u.kind], 1)

            def turn_y(now, s, u):
                pe.wait_ge(yn_ready[u.kind], u.count())
                turn_free(now, s, "y")
                pe.transpose(bank[:, TURN, 0:P], yn[u.buf][:, :], ident).then_inc(yT_ready[u.kind], 1)

            def logits(u):
                pe.wait_ge(x2_tile_ready, u.count())
                pe.matmul(bank[:, O_B, LG_COL:LG_COL + E], x2_tile[u.buf][:, :], rw[:, :], start=True, stop=True).then_inc(lg_ready, 1)

            def turn_comb(now, s, x):
                turn_free(now, s, "comb")
                pe.wait_ge(route, x.times(ROUTE_STEPS, ROUTE_STEPS))
                for t in range(MT):
                    last = pe.transpose(bank[0:E, TURN, t * P:(t + 1) * P], comb_new[:, t, :], ident)
                last.then_inc(ct_ready, 1)

            def out_bias(now, s, x):
                sums_free(now, s, "b2")
                pe.wait_ge(ct_done, x.times(1, 1))
                for t in range(MT):
                    last = pe.matmul(bank[:, Y_B, t * D:(t + 1) * D], combT[:, t * P:(t + 1) * P], b2[:, :],
                                     start=True, stop=True)
                last.then_inc(b2_ready, 1)

            def up(now, x, chunks):
                if x.e == 0 and chunks[0] == 0:
                    pe.wait_ge(x2_lo_ready, x.times(MT, MT))
                    if x.early(1):
                        pe.wait_ge(w1_lo_ready, E)
                        v = unit_at(now, -2)
                        pe.wait_ge(exp_done[v.kind], v.count())
                n = x.times(MB)
                hi, lo = [v[:, n:n + MB] if x.i is None else v[:, bass.ds(n, MB)] for v in (x2T_hi, x2T_lo)]
                for c in chunks:
                    if not (x.early(1) and c < 2):
                        pe.wait_ge(h_done, x.times(E * FC, x.e * FC + c - 1))
                    w = slice(c * P, (c + 1) * P)
                    for wt, src in ((w1_hi, hi), (w1_hi, lo), (w1_lo, hi)):
                        last = pe.matmul(bank[:, H_B + c % 2, :], wt[:, x.e, w], src, start=wt is w1_hi and src is hi,
                                         stop=wt is w1_lo)
                    last.then_inc(h_ready, 1)

            def down(now, s, x, tiles):
                if tiles[0] == 0:
                    if x.early(1):
                        pe.wait_ge(w2_in, 16)
                    pe.wait_ge(h_done, x.times(E * FC, x.e * FC + FC))
                    sums_free(now, s, "down")
                for t in tiles:
                    for c in range(FC):
                        last = pe.matmul(bank[:, Y_B, t * D:(t + 1) * D], hid[x.e % 2][:, c, t * P:(t + 1) * P],
                                         w2[:, x.e, c, :], start=c == 0, stop=c == FC - 1, skip_group_check=True)
                if tiles[-1] == MT - 1:
                    last.then_inc(y_ready, 1)

            def time(now):
                sa, ca = now.back(-1), now.back(1)
                for s in range(4):
                    x, y = expert_at(now, s), expert_at(now, s - 1)
                    if s == 0 and now.i is None and now.off == AHEAD - 1:
                        pe.wait_ge(moe_in, 48)
                        pe.transpose(bank[:, Y_B, 0:E * FC], b1_rows[:, :], ident[0:E * FC, 0:E * FC]).then_inc(b1_ready, 1)
                        pe.wait_ge(b1_done, 1)
                    if now.off == 0 and s == 2:
                        pe.wait_ge(w_in, 16 * WEIGHTS)
                    if now.off == 1 and s == 0:
                        pe.wait_ge(late_in, 16 * LATE_WEIGHTS)
                    if u := unit_at(now, s - 3):
                        turn_o(now, s, u)
                    if x:
                        up(now, x, (0, 1))
                    if u := unit_at(now, s):
                        scores(now, s, u)
                    u, v = unit_at(now, s - 2), unit_at(now, s - 5)
                    if u or v or unit_at(now, s - 3):
                        outs_free(now, s)
                    if v and v.kind == CROSS:
                        logits(v)
                    if u:
                        weigh(u)
                    if u := unit_at(now, s - 3):
                        out_proj(u)
                    if s == 0 and x and x.e == 0:
                        out_bias(now, s, x)
                    if x:
                        up(now, x, (2, 3))
                    if u := unit_at(now, s - 4):
                        turn_y(now, s, u)
                    if u := unit_at(now, s - 1):
                        scores_T(now, s, u)
                    if s == 0 and (sa.exists() or ca.exists()):
                        turn_free(now, s, "inputs")
                        if sa.exists():
                            turn_in(SELF, sa)
                        if ca.exists():
                            turn_in(CROSS, ca)
                    if s == 1 and sa.exists():
                        row_free(now, s)
                        pe.wait_ge(inT_done[SELF], sa.times(1, 1))
                        project(wq, inT[SELF][sa.par], q_ready, SELF)
                        project(wk, inT[SELF][sa.par], k_ready, SELF, 1)
                    if s == 2 and (sa.exists() or ca.exists()):
                        row_free(now, s)
                        if ca.exists():
                            pe.wait_ge(yT_done[SELF], ca.times(2, 2))
                            project(wq, x1T[ca.par], q_ready, CROSS)
                        if sa.exists():
                            v_proj(SELF, sa)
                    if s == 3 and ca.exists():
                        row_free(now, s)
                        pe.wait_ge(inT_done[CROSS], ca.times(1, 1))
                        project(wk, inT[CROSS][ca.par], k_ready, CROSS)
                        v_proj(CROSS, ca)
                    if y:
                        down(now, s, y, (0, 1))
                    if y:
                        down(now, s, y, (2, 3))
                    if s == 3 and (r := routed_at(now)):
                        turn_comb(now, s, r)

            schedule(pe, time)


_INS = ['x', 'ctx_1024', 'sa_wq', 'sa_bq', 'sa_wk', 'sa_bk', 'sa_wv', 'sa_bv', 'sa_wo', 'sa_bo', 'ca_wq', 'ca_bq', 'ca_wk',
        'ca_bk', 'ca_wv', 'ca_bv', 'ca_wo', 'ca_bo', 'ln1_g', 'ln1_b', 'ln2_g', 'ln2_b', 'ln3_g', 'ln3_b', 'router_w',
        'router_b', 'e_w1', 'e_b1', 'e_w2', 'e_b2']


def kernel(**inputs):
    import numpy as _np
    import concourse.bacc as _bacc
    from concourse import mybir as _mybir
    from concourse.bass_utils import run_bass_kernel_spmd as _run

    nc = _bacc.Bacc("TRN2", target_bir_lowering=False, num_devices=1)
    arrays, aps = {}, {}

    def give(name, a):
        arrays[f"in_{name}"] = _np.ascontiguousarray(a)
        aps[name] = nc.dram_tensor(f"in_{name}", a.shape, _mybir.dt.from_np(a.dtype), kind="ExternalInput").ap()

    for name in _INS:
        a = _np.asarray(inputs[name if name in ("x", "ctx_1024") else "L0_xattn_" + name])
        give(name, a.reshape(TOK, D) if name in ("x", "ctx_1024") else a)
    give("consts", shape_constants())
    out = nc.dram_tensor("out", (TOK, D), _mybir.dt.float32, kind="ExternalOutput").ap()
    build(nc, aps["x"], aps["ctx_1024"], aps["consts"], aps, out)
    r = _run(nc, [arrays], core_ids=[0])
    return r.results[0]["out"].reshape(B, S, D)
```
